# Optimizing a Trainium2 kernel written in Bass

```python
import numpy as np
import jax
import jax.numpy as jnp

def _softmax(x, axis=-1):
    return jax.nn.softmax(x, axis=axis)

def _gelu(x):
    return jax.nn.gelu(x, approximate=True)

def _silu(x):
    return jax.nn.silu(x)

def _sigmoid(x):
    return jax.nn.sigmoid(x)

def _layernorm(x, axis=-1, eps=1e-05):
    m = jnp.mean(x, axis=axis, keepdims=True)
    v = jnp.var(x, axis=axis, keepdims=True)
    return (x - m) / jnp.sqrt(v + eps)

def _scatter_add(tgt, idx, src, axis=0):
    return tgt.at[idx].add(src)

def _segment_sum(src, seg, n):
    return jax.ops.segment_sum(src, seg, n)
kernel_name = 'mk_xattn_seq_d2_seqx_r8_d2b663'

def setup_inputs(seed: int=0):
    np.random.seed(seed)
    _w = jnp.asarray

    def _rec_inputs():
        import jax
        import jax.numpy as jnp
        _rk = jax.random.key(seed)
        x = 7.22e-05 + 1 * jax.random.normal(jax.random.fold_in(_rk, 1), (32, 128, 128), jnp.float32)
        _lenS = 128 - jax.random.randint(jax.random.fold_in(_rk, 7), (32,), 0, max(1, 128 // 4) + 1, jnp.int32)
        _lenS2 = 128 - jax.random.randint(jax.random.fold_in(_rk, 8), (32,), 0, max(1, 128 // 4) + 1, jnp.int32)
        _ctx_1024P = jax.random.normal(jax.random.fold_in(_rk, 11), (32, 16, 128), jnp.float32)
        _ctx_1024c = jax.random.dirichlet(jax.random.fold_in(_rk, 511), 0.3 * jnp.ones((16,), jnp.float32), (32, 128))
        _ctx_1024t = jnp.einsum('bsk,bkd->bsd', _ctx_1024c, _ctx_1024P)
        _ctx_1024t = _ctx_1024t * jax.lax.rsqrt(jnp.mean(jnp.square(_ctx_1024t)) + 1e-12) * 0.953939
        ctx_1024 = 4.13588e-05 + 0.999923 * (_ctx_1024t + 0.3 * jax.random.normal(jax.random.fold_in(_rk, 611), (32, 128, 128), jnp.float32))
        itok_BxS_0_255 = jax.random.randint(jax.random.fold_in(_rk, 13), (32, 128), 0, 32, jnp.int32)
        _validS = jnp.arange(128)[None, :] < _lenS[:, None]
        _validS2 = jnp.arange(128)[None, :] < _lenS2[:, None]
        _causal = jnp.tril(jnp.ones((128, 128), dtype=bool))
        mask_BxS2_if1 = jnp.where(jnp.ones((32, 128), dtype=bool), 1, 0).astype(jnp.int32)
        return (x, ctx_1024, itok_BxS_0_255, mask_BxS2_if1)
    x, ctx_1024, itok_BxS_0_255, mask_BxS2_if1 = _rec_inputs()

    def _L0_xattn_setup():
        import jax, jax.numpy as jnp
        import numpy as np
        D_MODEL = 128
        N_HEADS = 16
        D_K = D_MODEL // N_HEADS
        key = jax.random.key(seed)
        ks = jax.random.split(key, 12)
        B, S, D = (4, 256, D_MODEL)
        scale = 1.0 / np.sqrt(D)
        inp = {'q': jax.random.normal(ks[0], (B, S, D), jnp.float32), 'k': jax.random.normal(ks[1], (B, S, D), jnp.float32), 'v': jax.random.normal(ks[2], (B, S, D), jnp.float32), 'mask': jnp.ones((B, S), jnp.int32), 'Wq': jax.random.normal(ks[3], (D, D), jnp.float32) * scale, 'bq': jnp.zeros((D,), jnp.float32), 'Wk': jax.random.normal(ks[4], (D, D), jnp.float32) * scale, 'bk': jnp.zeros((D,), jnp.float32), 'Wv': jax.random.normal(ks[5], (D, D), jnp.float32) * scale, 'bv': jnp.zeros((D,), jnp.float32), 'Wo': jax.random.normal(ks[6], (D, D), jnp.float32) * scale, 'bo': jnp.zeros((D,), jnp.float32), 'ln_gamma': jnp.ones((D,), jnp.float32), 'ln_beta': jnp.zeros((D,), jnp.float32)}
        return inp
    _L0_xattn_all = _L0_xattn_setup()
    _L0_xattn_in = {k: v for k, v in _L0_xattn_all.items() if k in ('Wq', 'bq', 'Wk', 'bk', 'Wv', 'bv', 'Wo', 'bo', 'ln_gamma', 'ln_beta')}
    del _L0_xattn_all

    def _L1_xattn_setup():
        import jax, jax.numpy as jnp
        import numpy as np
        import math
        EPS_RMS = 1.1920929e-07
        EPS_DEN = 1e-06

        def rmsnorm(x, gamma):
            ms = jnp.mean(x * x, axis=-1, keepdims=True)
            return x * jax.lax.rsqrt(ms + EPS_RMS) * gamma
        key = jax.random.key(seed)
        ks = jax.random.split(key, 8)
        B, T, K, D = (4, 512, 32, 128)
        x_tokens = jax.random.normal(ks[0], (B, T, D), dtype=jnp.float32)
        ctx = jax.random.normal(ks[1], (B, K, D), dtype=jnp.float32)
        idx = jnp.sort(jax.random.randint(ks[2], (B, T), 0, K), axis=-1)
        s = 1.0 / math.sqrt(D)
        Wq = jax.random.normal(ks[3], (D, D), dtype=jnp.float32) * s
        Wk = jax.random.normal(ks[4], (D, D), dtype=jnp.float32) * s
        Wv = jax.random.normal(ks[5], (D, D), dtype=jnp.float32) * s
        Wo = jax.random.normal(ks[6], (D, D), dtype=jnp.float32) * s
        return {'x_tokens': x_tokens, 'ctx': ctx, 'ctx_index_per_token': idx, 'gamma_q': jnp.ones((D,), jnp.float32), 'gamma_kv': jnp.ones((D,), jnp.float32), 'Wq': Wq, 'Wk': Wk, 'Wv': Wv, 'Wo': Wo}
    _L1_xattn_all = _L1_xattn_setup()
    _L1_xattn_in = {k: v for k, v in _L1_xattn_all.items() if k in ('gamma_q', 'gamma_kv', 'Wq', 'Wk', 'Wv', 'Wo')}
    del _L1_xattn_all
    return {'x': x, 'ctx_1024': ctx_1024, 'itok_BxS_0_255': itok_BxS_0_255, 'mask_BxS2_if1': mask_BxS2_if1, 'L0_xattn_Wq': _L0_xattn_in['Wq'], 'L0_xattn_bq': _L0_xattn_in['bq'], 'L0_xattn_Wk': _L0_xattn_in['Wk'], 'L0_xattn_bk': _L0_xattn_in['bk'], 'L0_xattn_Wv': _L0_xattn_in['Wv'], 'L0_xattn_bv': _L0_xattn_in['bv'], 'L0_xattn_Wo': _L0_xattn_in['Wo'], 'L0_xattn_bo': _L0_xattn_in['bo'], 'L0_xattn_ln_gamma': _L0_xattn_in['ln_gamma'], 'L0_xattn_ln_beta': _L0_xattn_in['ln_beta'], 'L1_xattn_gamma_q': _L1_xattn_in['gamma_q'], 'L1_xattn_gamma_kv': _L1_xattn_in['gamma_kv'], 'L1_xattn_Wq': _L1_xattn_in['Wq'], 'L1_xattn_Wk': _L1_xattn_in['Wk'], 'L1_xattn_Wv': _L1_xattn_in['Wv'], 'L1_xattn_Wo': _L1_xattn_in['Wo']}

def reference(x, ctx_1024, itok_BxS_0_255, mask_BxS2_if1, L0_xattn_Wq, L0_xattn_bq, L0_xattn_Wk, L0_xattn_bk, L0_xattn_Wv, L0_xattn_bv, L0_xattn_Wo, L0_xattn_bo, L0_xattn_ln_gamma, L0_xattn_ln_beta, L1_xattn_gamma_q, L1_xattn_gamma_kv, L1_xattn_Wq, L1_xattn_Wk, L1_xattn_Wv, L1_xattn_Wo):
    import jax
    import jax.numpy as jnp

    def _L0_xattn_ref(q, k, v, mask, Wq, bq, Wk, bk, Wv, bv, Wo, bo, ln_gamma, ln_beta):
        import jax, jax.numpy as jnp
        import numpy as np
        D_MODEL = 128
        N_HEADS = 16
        D_K = D_MODEL // N_HEADS
        B, S, D = q.shape
        H, dk = (N_HEADS, D_K)
        residual = q
        qh = (q @ Wq.T + bq).reshape(B, S, H, dk).transpose(0, 2, 1, 3)
        kh = (k @ Wk.T + bk).reshape(B, S, H, dk).transpose(0, 2, 1, 3)
        vh = (v @ Wv.T + bv).reshape(B, S, H, dk).transpose(0, 2, 1, 3)
        attn = jnp.einsum('bhqd,bhkd->bhqk', qh, kh) / jnp.sqrt(jnp.float32(dk))
        attn = jnp.where(mask[:, None, None, :] == 0, jnp.float32(-1000000000.0), attn)
        scores = jax.nn.softmax(attn, axis=-1)
        out = jnp.einsum('bhqk,bhkd->bhqd', scores, vh)
        out = out.transpose(0, 2, 1, 3).reshape(B, S, D)
        out = out @ Wo.T + bo
        x = out + residual
        mu = jnp.mean(x, axis=-1, keepdims=True)
        var = jnp.mean(jnp.square(x - mu), axis=-1, keepdims=True)
        return (x - mu) / jnp.sqrt(var + 1e-05) * ln_gamma + ln_beta

    def _L1_xattn_ref(x_tokens, ctx, ctx_index_per_token, gamma_q, gamma_kv, Wq, Wk, Wv, Wo):
        import jax, jax.numpy as jnp
        import numpy as np
        import math
        EPS_RMS = 1.1920929e-07
        EPS_DEN = 1e-06

        def rmsnorm(x, gamma):
            ms = jnp.mean(x * x, axis=-1, keepdims=True)
            return x * jax.lax.rsqrt(ms + EPS_RMS) * gamma
        B, T, D = x_tokens.shape
        K = ctx.shape[1]
        H = 16
        hd = D // H

        def split(x):
            return x.reshape(B, -1, H, hd).transpose(0, 2, 1, 3)
        q = split(rmsnorm(x_tokens, gamma_q) @ Wq.T)
        kn = rmsnorm(ctx, gamma_kv)
        k = split(kn @ Wk.T)
        v = split(kn @ Wv.T)
        ctx_pos = jnp.arange(K)[None, None, :]
        mask = (jnp.abs(ctx_pos - ctx_index_per_token[:, :, None]) <= 1)[:, None]
        scores = jnp.einsum('bhqd,bhkd->bhqk', q, k) / math.sqrt(hd)
        w = jnp.square(jax.nn.relu(scores))
        w = jnp.where(mask, w, 0.0)
        denom = jnp.maximum(w.sum(-1, keepdims=True), EPS_DEN)
        out = jnp.einsum('bhqk,bhkd->bhqd', w / denom, v)
        out = out.transpose(0, 2, 1, 3).reshape(B, T, D)
        return x_tokens + out @ Wo.T
    x = _L0_xattn_ref(x, ctx_1024, ctx_1024, mask_BxS2_if1, L0_xattn_Wq, L0_xattn_bq, L0_xattn_Wk, L0_xattn_bk, L0_xattn_Wv, L0_xattn_bv, L0_xattn_Wo, L0_xattn_bo, L0_xattn_ln_gamma, L0_xattn_ln_beta)
    x = _L1_xattn_ref(x, ctx_1024, itok_BxS_0_255, L1_xattn_gamma_q, L1_xattn_gamma_kv, L1_xattn_Wq, L1_xattn_Wk, L1_xattn_Wv, L1_xattn_Wo)
    return x

_drawn_inputs = setup_inputs


def setup_inputs(seed=0):
    import zlib

    import numpy as np

    out = dict(_drawn_inputs(seed))
    spreads = {'L0_xattn_bq': (0.0, 0.1),
     'L0_xattn_bk': (0.0, 0.1),
     'L0_xattn_bv': (0.0, 0.1),
     'L0_xattn_bo': (0.0, 0.1),
     'L0_xattn_ln_gamma': (1.0, 0.2),
     'L0_xattn_ln_beta': (0.0, 0.1),
     'L1_xattn_gamma_q': (1.0, 0.2),
     'L1_xattn_gamma_kv': (1.0, 0.2)}
    factors = {}
    for name, (base, spread) in spreads.items():
        noise = np.random.default_rng([zlib.crc32(name.encode()), seed]).standard_normal(out[name].shape)
        drawn = base * np.exp(spread * noise) if base else spread * noise
        out[name] = jnp.asarray(drawn.astype(out[name].dtype))
    for name, factor in factors.items():
        out[name] = (out[name] * factor).astype(out[name].dtype)
    return out
```

```python
from contextlib import ExitStack

import concourse.bass as bass
from concourse import mybir

ALU = mybir.AluOpType
ACT = mybir.ActivationFunctionType
AX = mybir.AxisListType
F32 = mybir.dt.float32
BF16 = mybir.dt.bfloat16
I32 = mybir.dt.int32

LN_EPS = 1e-5
RMS_EPS = 1.1920929e-07
DEN_EPS = 1e-6
MASKED = -1e9

GROUP = 4
UNROLL = 2 * GROUP
TERMS = 6
Q_RUNS = ((0, 3), (3, 2), (5, 1))
K_RUNS = ((0, 3), (3, 2), (5, 1))


class Step:

    def __init__(self, base, it=None):
        self.base, self.it = base, it
        self.s = base % GROUP

    def b(self, lag):
        return Count(self.base + lag, UNROLL, self.it)

    def g(self, lag):
        return Count(self.base // GROUP + lag, UNROLL // GROUP, self.it)


class Count:

    def __init__(self, first, stride, it):
        self.first, self.stride, self.it = first, stride, it

    def within(self, n):
        return 0 <= self.first < n

    def value(self, times=1, plus=0):
        v = self.first * times + plus
        if self.it is None:
            return max(v, 0)
        assert v > 0
        return v + self.it * (self.stride * times)

    def half(self):
        return Count(self.first // 2, self.stride // 2, self.it)


def xattn_kernel(nc, x, ctx, idx, mask, wq0, bq, wk0, bk, wv0, bv, wo0, bo, ln_g, ln_b,
                 gq, gkv, wq1, wk1, wv1, wo1, out):
    B, S, D = x.shape
    H = 16
    HD = D // H
    T = H // 2
    NG = B // GROUP
    GT = GROUP * S
    E_ROWS = TERMS * HD
    MASK_ROW = 2 * E_ROWS
    M_ROW = MASK_ROW + 1
    A_ROWS = MASK_ROW + 1
    B_ROWS = M_ROW + 2
    CH = 4
    SCALE = float(HD) ** -0.5
    P = 128
    assert S == P and D == P and NG >= 8 and NG % 2 == 0

    es = ExitStack()
    with es:
        def sb(name, shape, dt=F32):
            return es.enter_context(nc.sbuf_tensor(name, shape, dt))

        def sem(name):
            return es.enter_context(nc.semaphore(name))

        def sems(name, n):
            return [sem(f"{name}{i}") for i in range(n)]

        q_scr = [nc.dram_tensor(f"q_scr{i}", [2, TERMS, HD * T, GT], BF16).ap() for i in range(2)]
        k_scr = [nc.dram_tensor(f"k_scr{i}", [2, TERMS, HD * T, GT], BF16).ap() for i in range(2)]

        ident = sb("ident", [P, P])
        w_raw = sb("w_raw", [P, 8, P])
        wqT = sb("wqT", [P, P])
        wkT = sb("wkT", [P, P])
        wvkT = sb("wvkT", [P, 3, P])
        woT = sb("woT", [P, P])
        wq1T = sb("wq1T", [P, P])
        wo1T = sb("wo1T", [P, P])
        cols = sb("cols", [P, 5])
        rows_bc = sb("rows_bc", [P, 3, P])
        bv_rep = sb("bv_rep", [P, P])
        c0 = sb("c0", [P, P])
        pos = sb("pos", [P, 3])
        m_half = sb("m_half", [P, GROUP])
        eps = sb("eps", [P, GROUP + 2])

        xg = [sb(f"xg{i}", [P, GROUP, P]) for i in range(2)]
        cg = [sb(f"cg{i}", [P, GROUP, P]) for i in range(2)]
        xres = [sb(f"xres{i}", [P, GROUP, P]) for i in range(2)]
        maskb = [sb(f"maskb{i}", [P, GT], I32) for i in range(2)]
        idxb = [sb(f"idxb{i}", [P, GT], I32) for i in range(2)]
        onehot = [sb(f"onehot{i}", [P, 3, GT]) for i in range(2)]
        keep = sb("keep", [P, GT])
        mrow = sb("mrow", [1, GT], BF16)
        xT = sb("xT", [P, GT])
        cT = [sb(f"cT{i}", [P, GT]) for i in range(2)]
        q3 = sb("q3", [P, 3, GT], BF16)
        k3 = sb("k3", [P, 3, GT], BF16)
        rq = sb("rq", [P, GT])
        kf = sb("kf", [P, GT])
        rk = sb("rk", [P, GT])
        qst = [sb(f"qst{i}", [P, T, 2, GT], BF16) for i in range(2)]
        kst = [sb(f"kst{i}", [P, T, GT], BF16) for i in range(2)]
        cssq = [sb(f"cssq{i}", [P, GROUP]) for i in range(2)]
        cms = sb("cms", [P, GROUP])
        crs = [sb(f"crs{i}", [P, GROUP]) for i in range(2)]
        outg = [sb(f"outg{i}", [P, GROUP, P]) for i in range(2)]

        vpad = [sb(f"vpad{i}", [P, H, 32]) for i in range(2)]
        kv1 = [sb(f"kv1_{i}", [P, 2 * P]) for i in range(4)]
        negmax = sb("negmax", [P, H])
        m_hi = sb("m_hi", [H, P], BF16)
        m_lo = sb("m_lo", [H, P], BF16)
        probs = [sb(f"probs{i}", [P, CH, 4 * P]) for i in range(2)]
        pvs = sb("pvs", [P, 2, P])
        rden = sb("rden", [P, T, 2])
        on = sb("on", [P, P])
        onT = sb("onT", [P, P])
        xb = [sb(f"xb{i}", [P, P]) for i in range(2)]
        y = sb("y", [P, P])
        bn = sb("bn", [P, 6])
        mv = sb("mv", [P, 2])
        ve = sb("ve", [P, 1])
        rstd = sb("rstd", [P, 1])
        t1 = sb("t1", [P, P])
        t2 = sb("t2", [P, P])
        x1 = [sb(f"x1_{i}", [P, P]) for i in range(4)]
        sq_c = sb("sq_c", [P, P])
        sq_x = sb("sq_x", [P, P])
        xssq = sb("xssq", [P, 1])
        xms = sb("xms", [P, 1])
        xrs = [sb(f"xrs{i}", [P, 1]) for i in range(2)]
        x1T = sb("x1T", [P, P])
        q1 = sb("q1", [P, P])
        prodk = sb("prodk", [P, 3 * H, HD])
        s48 = sb("s48", [P, 3 * H])
        r48 = sb("r48", [P, 3 * H])
        w48 = sb("w48", [P, 3, H])
        den = sb("den", [P, H])
        denm = sb("denm", [P, H])
        rec = sb("rec", [P, H])
        wn = sb("wn", [P, 3, H])
        prodv = sb("prodv", [P, 3, P])
        o1 = sb("o1", [P, P])
        o1T = sb("o1T", [P, P])

        def bank(name):
            return es.enter_context(nc.psum_tensor(name, [P, 512], F32))

        ps_a = [bank("ps_a0"), bank("ps_a1")]
        ps_b = [bank("ps_b0"), bank("ps_b1")]
        ps_tok = bank("ps_tok")
        ps_prep = bank("ps_prep")
        ps_l1 = bank("ps_l1")
        ps_sel = bank("ps_sel")

        w_in, cols_in, rows_in = sem("w_in"), sem("cols_in"), sem("rows_in")
        pool_setup, ident_ok, stacks_ok = sem("pool_setup"), sem("ident_ok"), sem("stacks_ok")
        wt_ps, wt_ok, bv_ok, c0_ps, c0_ok = sem("wt_ps"), sem("wt_ok"), sem("bv_ok"), sem("c0_ps"), sem("c0_ok")
        x_in, c_in, mask_in = sems("x_in", 2), sems("c_in", 2), sems("mask_in", 2)
        idx_in, xres_in = sems("idx_in", 2), sems("xres_in", 2)
        xT_ps, xT_ok, q_ps, q_hi, q_r, q_mid, q_lo = [sem(n) for n in ("xT_ps", "xT_ok", "q_ps", "q_hi", "q_r", "q_mid", "q_lo")]
        cT_ps, cT_ok, k_ps, k_f, k_hi, k_r, k_mid, k_lo = [sem(n) for n in ("cT_ps", "cT_ok", "k_ps", "k_f", "k_hi", "k_r", "k_mid", "k_lo")]
        keep_ok, mrow_ok = sem("keep_ok"), sem("mrow_ok")
        q_written, k_written = sem("q_written"), sem("k_written")
        q_stacked, k_stacked = sems("q_stacked", 2), sems("k_stacked", 2)
        cssq_ok, cms_ok, crs_ok, onehot_ok = sem("cssq_ok"), sem("cms_ok"), sem("crs_ok"), sem("onehot_ok")
        vkv_ps, v_ok, kv1_ok = sem("vkv_ps"), sem("v_ok"), sem("kv1_ok")
        a_ps, a_max, mT_ps, m_hi_ok, m_lo_ok, m_stacked = [sem(n) for n in ("a_ps", "a_max", "mT_ps", "m_hi_ok", "m_lo_ok", "m_stacked")]
        b_ps, exp_ok, pv_ps, pvs_ok = sem("b_ps"), sem("exp_ok"), sem("pv_ps"), sem("pvs_ok")
        tok_ps, rden_ok, on_ok, onT_ps, onT_ok, wo_ps = [sem(n) for n in ("tok_ps", "rden_ok", "on_ok", "onT_ps", "onT_ok", "wo_ps")]
        xb_ok, y_ok, bn_ok, mv_ok, ve_ok, rstd_ok, t1_ok, t2_ok, x1_ok = [sem(n) for n in (
            "xb_ok", "y_ok", "bn_ok", "mv_ok", "ve_ok", "rstd_ok", "t1_ok", "t2_ok", "x1_ok")]
        xssq_ok, xms_ok, xrs_ok = sem("xssq_ok"), sem("xms_ok"), sem("xrs_ok")
        x1T_ps, x1T_ok, q1_ps, q1_ok = sem("x1T_ps"), sem("x1T_ok"), sem("q1_ps"), sem("q1_ok")
        selk_ps, prodk_ok, s48_ok, r48_ok, w48_ok, den_ok, denm_ok, rec_ok, wn_ok = [sem(n) for n in (
            "selk_ps", "prodk_ok", "s48_ok", "r48_ok", "w48_ok", "den_ok", "denm_ok", "rec_ok", "wn_ok")]
        selv_ps, prodv_ok, o1_ok, o1T_ps, o1T_ok, wo1_ps, out_ok = [sem(n) for n in (
            "selv_ps", "prodv_ok", "o1_ok", "o1T_ps", "o1T_ok", "wo1_ps", "out_ok")]
        out_stored = sems("out_stored", 2)

        FIRST, LOOP, LAST = -2 * GROUP, UNROLL, B + GROUP
        LOOPS = (B - 2 * GROUP - LOOP) // UNROLL

        def run(eng, step):
            for n in range(FIRST, LOOP):
                step(Step(n))
            with eng.Fori(0, LOOPS) as it:
                for s in range(UNROLL):
                    step(Step(LOOP + s, it))
            for n in range(LOOP + LOOPS * UNROLL, LAST):
                step(Step(n))

        def rows_of(tensor, g):
            at = g.value(GROUP)
            part = tensor[at:at + GROUP] if g.it is None else tensor[bass.ds(at, GROUP)]
            return part.rearrange("b s d -> s b d")

        def bcast_of(tensor, g):
            at = g.value(GT)
            flat = tensor.rearrange("(a b) s -> a (b s)", a=1)
            part = flat[:, at:at + GT] if g.it is None else flat[:, bass.ds(at, GT)]
            return part.to_broadcast([P, GT])

        block = es.enter_context(nc.Block())

        @block.sync
        def _(sp):
            for i, w in enumerate((wq0, wk0, wv0, wk1, wv1, wo0, wq1, wo1)):
                sp.dma_start(w_raw[:, i, :], w).then_inc(w_in, 16)
            for c, b in ((0, bq), (1, bk)):
                for e in range(2):
                    with nc.allow_non_contiguous_dma("a bias of 128 numbers, once"):
                        src = b.rearrange("(t e d) -> e d t", e=2, d=HD)[e]
                        sp.dma_start(cols[64 * e:64 * e + 64, c:c + 1], src).then_inc(cols_in, 16)
            for c, v in ((2, bv), (3, gq), (4, gkv)):
                with nc.allow_non_contiguous_dma("a vector of 128 numbers, once"):
                    sp.dma_start(cols[:, c:c + 1], v.rearrange("(p a) -> p a", a=1)).then_inc(cols_in, 16)
            for c, v in enumerate((bo, ln_g, ln_b)):
                sp.dma_start(rows_bc[:, c, :], v.rearrange("(a n) -> a n", a=1).to_broadcast([P, P])).then_inc(rows_in, 16)

            def write_scratch(scr, parts, runs, repeat, done):
                for e in range(2):
                    dst = scr[e].rearrange("t r n -> r t n")
                    for i, (t0, n) in enumerate(runs):
                        src = (parts[64 * e:64 * e + 64, i:i + 1, :].to_broadcast([64, n, GT]) if repeat
                               else parts[64 * e:64 * e + 64, 0:n, :])
                        sp.dma_start(dst[:, t0:t0 + n, :], src).then_inc(done, 16)

            sp.wait_ge(stacks_ok, 1)

            def step(st):
                s = st.s
                g = st.g(2)
                p = g.first % 2
                if s == 0 and g.within(NG):
                    sp.dma_start(xg[p][:, :, :], rows_of(x, g)).then_inc(x_in[p], 16)
                    sp.dma_start(cg[p][:, :, :], rows_of(ctx, g)).then_inc(c_in[p], 16)
                    sp.dma_start(maskb[p][:, :], bcast_of(mask, g)).then_inc(mask_in[p], 16)
                b, g = st.b(1), st.g(1)
                if b.within(B):
                    qs = qst[(b.first // GROUP) % 2]
                    at = (b.first % GROUP) * S
                    for i, (m, ok) in enumerate(((m_hi, m_hi_ok), (m_lo, m_lo_ok))):
                        if i == 1 and s == 0 and g.within(NG):
                            sp.wait_ge(q_written, g.value(96, 96))
                        sp.wait_ge(ok, b.value(plus=1))
                        sp.dma_start(qs[M_ROW + i:M_ROW + i + 1, :, :, at:at + S].rearrange("p t e n -> p (t e) n"),
                                     m[:, :]).then_inc(m_stacked, 16)
                p = g.first % 2
                if s == 0 and g.within(NG):
                    if not b.within(B):
                        sp.wait_ge(q_written, g.value(96, 96))
                    sp.wait_ge(b_ps, g.value(4 * GROUP, -4 * GROUP))
                    for e in range(2):
                        sp.dma_start(qst[p][E_ROWS * e:E_ROWS * (e + 1), :, e, :],
                                     q_scr[p][e].rearrange("t (d a) n -> (t d) a n", a=T)).then_inc(q_stacked[p], 16)
                    sp.wait_ge(k_lo, g.value(plus=1))
                    write_scratch(k_scr[p], k3, K_RUNS, False, k_written)
                if s == 1 and g.within(NG):
                    sp.wait_ge(k_written, g.value(96, 96))
                    sp.wait_ge(mrow_ok, g.value(plus=1))
                    sp.dma_start(kst[p][0:2 * E_ROWS, :, :].rearrange("p t n -> p (t n)"),
                                 k_scr[p].rearrange("e t (d a) n -> (e t d) (a n)", a=T)).then_inc(k_stacked[p], 16)
                    sp.dma_start(kst[p][MASK_ROW:MASK_ROW + 1, :, :],
                                 mrow[0:1, None, :].to_broadcast([1, T, GT])).then_inc(k_stacked[p], 16)
                g = st.g(2)
                p = g.first % 2
                if s == 2 and g.within(NG):
                    sp.wait_ge(q_lo, g.value(plus=1))
                    write_scratch(q_scr[p], q3, Q_RUNS, True, q_written)
                if s == 3 and g.within(NG):
                    sp.wait_ge(onehot_ok, g.value(plus=-1))
                    sp.dma_start(idxb[p][:, :], bcast_of(idx, g)).then_inc(idx_in[p], 16)
                g = st.g(1)
                if s == 2 and g.within(NG):
                    sp.wait_ge(xb_ok, g.value(GROUP, -GROUP))
                    sp.dma_start(xres[g.first % 2][:, :, :], rows_of(x, g)).then_inc(xres_in[g.first % 2], 16)
                g = st.g(-1)
                if s == 3 and g.within(NG):
                    sp.wait_ge(out_ok, g.value(GROUP, GROUP))
                    sp.dma_start(rows_of(out, g), outg[g.first % 2][:, :, :]).then_inc(out_stored[g.first % 2], 16)

            run(sp, step)
            for p in range(2):
                sp.wait_ge(out_stored[p], 16 * (NG // 2))

        @block.gpsimd
        def _(pool):
            setup = [0]

            def alone(ins):
                ins.then_inc(pool_setup, 1)
                setup[0] += 1
                pool.wait_ge(pool_setup, setup[0])

            alone(pool.memset(ident[:, :], 0.0))
            pool.affine_select(out=ident[:, :], in_=ident[:, :], compare_op=ALU.not_equal, fill=1.0,
                               base=0, pattern=[[-1, P]], channel_multiplier=1).then_inc(ident_ok, 1)
            alone(pool.iota(pos[:, :], pattern=[[-1, 3]], base=1, channel_multiplier=1,
                            allow_small_or_imprecise_dtypes=True))
            alone(pool.memset(eps[:, 0:GROUP], RMS_EPS))
            alone(pool.memset(eps[:, GROUP:GROUP + 1], HD * RMS_EPS))
            alone(pool.memset(eps[:, GROUP + 1:GROUP + 2], LN_EPS))
            alone(pool.memset(m_half[:, :], -0.5))
            for i in range(2):
                alone(pool.memset(qst[i][:, :, :, :].rearrange("p t e n -> p (t e n)").bitcast(F32), 0.0))
                alone(pool.memset(qst[i][MASK_ROW:MASK_ROW + 1, :, :, :], 1.0))
                alone(pool.memset(kst[i][MASK_ROW:P, :, :], 1.0))
            for i in range(2):
                alone(pool.memset(vpad[i][:, :, :], 0.0))
                for e in range(2):
                    v = vpad[i][:, :, :].rearrange("p (t e) c -> p t e c", e=2)
                    alone(pool.memset(v[:, :, e, 16 + HD * e:16 + HD * (e + 1)], 1.0))
            pool.sem_inc(stacks_ok, 1)

            def power(dst, base, n, ok):
                return pool.tensor_tensor(dst, base, m_half[:, 0:n], ALU.pow).then_inc(ok, 1)

            def step(st):
                s = st.s
                g1 = st.g(1)
                p1 = g1.first % 2
                if s == 2 and g1.within(NG):
                    pool.wait_ge(idx_in[p1], g1.half().value(16, 16))
                    pool.wait_ge(selv_ps, g1.value(GROUP, -GROUP))
                b = st.b(0)
                if b.within(B):
                    g = st.g(0)
                    if s == 0:
                        pool.wait_ge(xres_in[g.first % 2], g.half().value(16, 16))
                    if b.first == 0:
                        pool.wait_ge(c0_ok, 1)
                    pool.wait_ge(y_ok, b.value(plus=-1))
                    pool.tensor_tensor(xb[b.first % 2][:, :], xres[g.first % 2][:, s, :], c0[:, :], ALU.add).then_inc(xb_ok, 1)
                if s == 2 and g1.within(NG):
                    for j in range(3):
                        last = pool.tensor_scalar(onehot[p1][:, j, :], idxb[p1][:, :], pos[:, j:j + 1], None, ALU.is_equal)
                    last.then_inc(onehot_ok, 1)
                g = st.g(1)
                p = g.first % 2
                if s == 0 and g.within(NG):
                    pool.wait_ge(k_hi, g.value(plus=1))
                    pool.wait_ge(k_mid, g.value())
                    pool.tensor_tensor(rk[:, :], kf[:, :], k3[:, 0, :], ALU.subtract).then_inc(k_r, 1)
                    pool.wait_ge(cssq_ok, g.value(GROUP, GROUP))
                    pool.tensor_tensor(cms[:, :], cssq[p][:, :], eps[:, 0:GROUP], ALU.add).then_inc(cms_ok, 1)
                    pool.wait_ge(cms_ok, g.value(plus=1))
                    pool.wait_ge(kv1_ok, g.value(GROUP, -GROUP))
                    power(crs[p][:, :], cms[:, :], GROUP, crs_ok)
                b = st.b(-2)
                if b.within(B):
                    pool.wait_ge(xssq_ok, b.value(plus=1))
                    pool.tensor_tensor(xms[:, :], xssq[:, :], eps[:, GROUP:GROUP + 1], ALU.add).then_inc(xms_ok, 1)
                    pool.wait_ge(xms_ok, b.value(plus=1))
                    pool.wait_ge(r48_ok, b.value(plus=-1))
                    power(xrs[b.first % 2][:, :], xms[:, :], 1, xrs_ok)
                if s == 0 and g.within(NG):
                    pool.wait_ge(k_mid, g.value(plus=1))
                    pool.tensor_tensor(k3[:, 2, :], rk[:, :], k3[:, 1, :], ALU.subtract).then_inc(k_lo, 1)
                g = st.g(2)
                p = g.first % 2
                if s == 2 and g.within(NG):
                    pool.wait_ge(q_mid, g.value(plus=1))
                    pool.tensor_tensor(q3[:, 2, :], rq[:, :], q3[:, 1, :], ALU.subtract).then_inc(q_lo, 1)
                b = st.b(-1)
                if b.within(B):
                    pool.wait_ge(mv_ok, b.value(plus=1))
                    pool.tensor_tensor(ve[:, :], mv[:, 1:2], eps[:, GROUP + 1:GROUP + 2], ALU.add).then_inc(ve_ok, 1)
                    pool.wait_ge(ve_ok, b.value(plus=1))
                    pool.wait_ge(t1_ok, b.value())
                    power(rstd[:, :], ve[:, :], 1, rstd_ok)
                    pool.wait_ge(t1_ok, b.value(plus=1))
                    pool.tensor_tensor(t2[:, :], t1[:, :], rows_bc[:, 1, :], ALU.mult).then_inc(t2_ok, 1)
                    pool.wait_ge(t2_ok, b.value(plus=1))
                    pool.wait_ge(out_ok, b.value(plus=-3))
                    pool.tensor_tensor(x1[b.first % 4][:, :], t2[:, :], rows_bc[:, 2, :], ALU.add).then_inc(x1_ok, 1)

            run(pool, step)

        @block.tensor
        def _(pe):
            pe.wait_ge(ident_ok, 1)
            pe.wait_ge(w_in, 16 * 8)
            for i in range(8):
                ps = (ps_a[0], ps_a[1])[i // 4]
                last = nc.tensor.transpose(ps[:, (i % 4) * P:(i % 4 + 1) * P], w_raw[:, i, :], ident[:, :])
                if i % 4 == 3:
                    last.then_inc(wt_ps, 1)
            pe.wait_ge(wt_ok, 2)
            pe.wait_ge(bv_ok, 1)
            nc.tensor.matmul(ps_tok[:, 0:P], bv_rep[:, :], woT[:, :], start=True, stop=True).then_inc(c0_ps, 1)
            pe.wait_ge(c0_ok, 1)
            pe.wait_ge(stacks_ok, 1)

            def step(st):
                s = st.s
                cur, ahead, after = st.b(0), st.b(2), st.b(-1)

                def scores_kq(c):
                    if not cur.within(B):
                        return
                    p, at = (cur.first // GROUP) % 2, s * S
                    if c == 0:
                        pe.wait_ge(m_stacked, cur.value(32, 32))
                    pe.wait_ge(exp_ok, cur.value(4, c - 1))
                    for i in range(2):
                        t = 2 * c + i
                        last = nc.tensor.matmul(ps_b[c % 2][:, 2 * P * i:2 * P * (i + 1)],
                                                kst[p][0:B_ROWS, t, at:at + S],
                                                qst[p][0:B_ROWS, t, :, at:at + S], start=True, stop=True)
                    last.then_inc(b_ps, 1)

                def scores_qk(c):
                    if not ahead.within(B):
                        return
                    p, at = (ahead.first // GROUP) % 2, (ahead.first % GROUP) * S
                    if c == 0 and at == 0:
                        gh = st.g(1).half()
                        pe.wait_ge(q_stacked[p], gh.value(32, 32))
                        pe.wait_ge(k_stacked[p], gh.value(32, 32))
                    if c == 0:
                        pe.wait_ge(m_hi_ok, ahead.value())
                        pe.wait_ge(m_lo_ok, ahead.value())
                    else:
                        pe.wait_ge(a_max, ahead.value(4, 0 if c == 1 else c - 1))
                    for h in range(4 * c, 4 * c + 4):
                        t, e = h // 2, h % 2
                        last = nc.tensor.matmul(ps_a[c % 2][:, (h % 4) * P:(h % 4 + 1) * P],
                                                qst[p][0:A_ROWS, t, e, at:at + S],
                                                kst[p][0:A_ROWS, t, at:at + S], start=True, stop=True)
                    last.then_inc(a_ps, 1)

                def max_rows():
                    if ahead.within(B):
                        pe.wait_ge(a_max, ahead.value(4, 4))
                        nc.tensor.matmul(ps_a[0][0:H, 0:P], negmax[:, :], ident[:, :], start=True, stop=True).then_inc(mT_ps, 1)

                def values():
                    if not cur.within(B):
                        return
                    pe.wait_ge(v_ok, cur.value(plus=1))
                    pe.wait_ge(y_ok, cur.value())
                    for half in range(2):
                        pe.wait_ge(exp_ok, cur.value(4, 2 * half + 2))
                        for e in range(2):
                            for j in range(4):
                                h = 8 * half + 2 * j + e
                                last = nc.tensor.matmul(ps_tok[32 * j:32 * j + 32, P * half:P * (half + 1)],
                                                        vpad[cur.first % 2][:, h, :],
                                                        probs[cur.first % 2][:, h // 4, (h % 4) * P:(h % 4 + 1) * P],
                                                        start=(e == 0), stop=(e == 1))
                    last.then_inc(pv_ps, 1)

                def to_tokens():
                    if after.within(B):
                        pe.wait_ge(pvs_ok, after.value(plus=1))
                        for half in range(2):
                            last = nc.tensor.transpose(ps_tok[:, P * half:P * (half + 1)], pvs[:, half, :], ident[:, :])
                        last.then_inc(tok_ps, 1)

                def to_features():
                    if after.within(B):
                        pe.wait_ge(on_ok, after.value(plus=1))
                        nc.tensor.transpose(ps_tok[:, 0:P], on[:, :], ident[:, :]).then_inc(onT_ps, 1)

                def out_proj0():
                    if after.within(B):
                        pe.wait_ge(onT_ok, after.value(plus=1))
                        nc.tensor.matmul(ps_tok[:, 0:P], onT[:, :], woT[:, :], start=True, stop=True).then_inc(wo_ps, 1)

                def l1_transpose():
                    b = st.b(-2)
                    if b.within(B):
                        pe.wait_ge(x1_ok, b.value(plus=1))
                        pe.wait_ge(out_ok, b.value(plus=-1))
                        nc.tensor.transpose(ps_l1[:, 0:P], x1[b.first % 4][:, :], ident[:, :]).then_inc(x1T_ps, 1)

                def l1_query():
                    b = st.b(-2)
                    if b.within(B):
                        pe.wait_ge(x1T_ok, b.value(plus=1))
                        nc.tensor.matmul(ps_l1[:, 0:P], x1T[:, :], wq1T[:, :], start=True, stop=True).then_inc(q1_ps, 1)

                def select(which, done):
                    b = st.b(-2)
                    if not b.within(B):
                        return
                    i = b.first % GROUP
                    if which == 0:
                        if i == 0:
                            pe.wait_ge(onehot_ok, st.g(0).value(plus=1))
                        pe.wait_ge(kv1_ok, b.value(plus=1))
                        pe.wait_ge(prodv_ok, b.value())
                    else:
                        pe.wait_ge(prodk_ok, b.value(plus=1))
                    for j in range(3):
                        last = nc.tensor.matmul(ps_sel[:, P * j:P * (j + 1)],
                                                onehot[(b.first // GROUP) % 2][:, j, i * S:(i + 1) * S],
                                                kv1[b.first % 4][:, P * which:P * (which + 1)], start=True, stop=True)
                    last.then_inc(done, 1)

                def l1_out_transpose():
                    b = st.b(-3)
                    if b.within(B):
                        pe.wait_ge(o1_ok, b.value(plus=1))
                        if st.b(-2).within(B):
                            pe.wait_ge(q1_ok, st.b(-2).value(plus=1))
                        else:
                            pe.wait_ge(out_ok, b.value())
                        nc.tensor.transpose(ps_l1[:, 0:P], o1[:, :], ident[:, :]).then_inc(o1T_ps, 1)

                def l1_out_proj():
                    b = st.b(-3)
                    if b.within(B):
                        pe.wait_ge(o1T_ok, b.value(plus=1))
                        nc.tensor.matmul(ps_l1[:, 0:P], o1T[:, :], wo1T[:, :], start=True, stop=True).then_inc(wo1_ps, 1)

                def project_ctx():
                    b = st.b(1)
                    if not b.within(B):
                        return
                    i, p = b.first % GROUP, (b.first // GROUP) % 2
                    gb = Step(st.base - 1, st.it).g(2)
                    if gb.within(NG):
                        ps = (s - 1) % GROUP
                        pe.wait_ge((xT_ok, q_r, cT_ok, k_f)[ps], gb.value(plus=1))
                    nc.tensor.matmul(ps_prep[:, 0:3 * P], cT[p][:, i * S:(i + 1) * S],
                                     wvkT[:, :, :], start=True, stop=True).then_inc(vkv_ps, 1)

                def group_piece():
                    g = st.g(2)
                    if not g.within(NG):
                        return
                    p = g.first % 2
                    if st.b(1).within(B):
                        pe.wait_ge(kv1_ok, st.b(1).value(plus=1))
                    if s == 0:
                        pe.wait_ge(x_in[p], g.half().value(16, 16))
                        pe.wait_ge(k_f, g.value())
                        for i in range(GROUP):
                            last = nc.tensor.transpose(ps_prep[:, P * i:P * (i + 1)], xg[p][:, i, :], ident[:, :])
                        last.then_inc(xT_ps, 1)
                    elif s == 1:
                        pe.wait_ge(xT_ok, g.value(plus=1))
                        nc.tensor.matmul(ps_prep[:, :], wqT[:, :], xT[:, :], start=True, stop=True).then_inc(q_ps, 1)
                    elif s == 2:
                        pe.wait_ge(c_in[p], g.half().value(16, 16))
                        pe.wait_ge(q_r, g.value(plus=1))
                        for i in range(GROUP):
                            last = nc.tensor.transpose(ps_prep[:, P * i:P * (i + 1)], cg[p][:, i, :], ident[:, :])
                        last.then_inc(cT_ps, 1)
                    else:
                        pe.wait_ge(cT_ok, g.value(plus=1))
                        nc.tensor.matmul(ps_prep[:, :], wkT[:, :], cT[p][:, :], start=True, stop=True).then_inc(k_ps, 1)

                scores_kq(0)
                scores_qk(0)
                l1_transpose()
                scores_kq(1)
                scores_qk(1)
                to_tokens()
                l1_query()
                scores_kq(2)
                scores_qk(2)
                to_features()
                select(0, selk_ps)
                scores_kq(3)
                scores_qk(3)
                l1_out_transpose()
                out_proj0()
                project_ctx()
                select(1, selv_ps)
                l1_out_proj()
                group_piece()
                max_rows()
                values()

            run(pe, step)

        @block.scalar
        def _(act):
            act.wait_ge(cols_in, 16 * 7)
            act.wait_ge(stacks_ok, 1)
            act.wait_ge(wt_ps, 1)
            perm = "p (t e d) -> p t e d"
            for w, i in ((wqT, 0), (wkT, 1)):
                act.activation(w[:, :].rearrange("p (e d t) -> p t e d", e=2, d=HD),
                               ps_a[0][:, i * P:(i + 1) * P].rearrange(perm, e=2, d=HD), ACT.Copy)
            act.activation(wvkT[:, 0, :], ps_a[0][:, 2 * P:3 * P], ACT.Copy)
            act.activation(wvkT[:, 1, :], ps_a[0][:, 3 * P:4 * P], ACT.Copy, scale=cols[:, 4:5]).then_inc(wt_ok, 1)
            act.wait_ge(wt_ps, 2)
            act.activation(wvkT[:, 2, :], ps_a[1][:, 0:P], ACT.Copy, scale=cols[:, 4:5])
            act.activation(woT[:, :], ps_a[1][:, P:2 * P], ACT.Copy)
            act.activation(wq1T[:, :], ps_a[1][:, 2 * P:3 * P], ACT.Copy, scale=cols[:, 3:4])
            act.activation(wo1T[:, :], ps_a[1][:, 3 * P:4 * P], ACT.Copy).then_inc(wt_ok, 1)

            def step(st):
                s = st.s
                cur = st.b(0)

                def exps(c):
                    if cur.within(B):
                        act.wait_ge(b_ps, cur.value(4, c + 1))
                        if c == 0:
                            act.wait_ge(pv_ps, cur.value(plus=-1))
                        act.activation(probs[cur.first % 2][:, c, :], ps_b[c % 2][:, :], ACT.Exp, scale=SCALE).then_inc(exp_ok, 1)

                b = st.b(-1)
                if b.within(B):
                    act.wait_ge(pv_ps, b.value(plus=1))
                    act.wait_ge(tok_ps, b.value())
                    act.activation(pvs[:, :, :].rearrange("p a n -> p (a n)"), ps_tok[:, 0:2 * P], ACT.Copy).then_inc(pvs_ok, 1)
                g = st.g(1)
                if s == 0 and g.within(NG):
                    act.wait_ge(k_r, g.value(plus=1))
                    act.wait_ge(k_written, g.value(96))
                    act.activation(k3[:, 1, :], rk[:, :], ACT.Copy).then_inc(k_mid, 1)
                g = st.g(2)
                if s == 2 and g.within(NG):
                    act.wait_ge(q_r, g.value(plus=1))
                    act.activation(q3[:, 1, :], rq[:, :], ACT.Copy).then_inc(q_mid, 1)
                exps(0)
                b = st.b(-2)
                if b.within(B):
                    act.wait_ge(x1T_ps, b.value(plus=1))
                    act.wait_ge(q1_ps, b.value())
                    act.activation(x1T[:, :], ps_l1[:, 0:P], ACT.Copy).then_inc(x1T_ok, 1)
                exps(1)
                if b.within(B):
                    act.wait_ge(q1_ps, b.value(plus=1))
                    act.wait_ge(prodk_ok, b.value())
                    act.activation(q1[:, :], ps_l1[:, 0:P], ACT.Copy).then_inc(q1_ok, 1)
                exps(2)
                b = st.b(-1)
                if b.within(B):
                    act.wait_ge(onT_ps, b.value(plus=1))
                    act.wait_ge(wo_ps, b.value())
                    act.activation(onT[:, :], ps_tok[:, 0:P], ACT.Copy).then_inc(onT_ok, 1)
                exps(3)
                b = st.b(-3)
                if b.within(B):
                    act.wait_ge(o1T_ps, b.value(plus=1))
                    act.wait_ge(wo1_ps, b.value())
                    act.activation(o1T[:, :], ps_l1[:, 0:P], ACT.Copy).then_inc(o1T_ok, 1)
                g = st.g(2)
                if g.within(NG):
                    p = g.first % 2
                    if s == 0:
                        act.wait_ge(c_in[p], g.half().value(16, 16))
                        act.wait_ge(cms_ok, g.value(plus=-1))
                    act.wait_ge(cssq_ok, g.value(GROUP, s))
                    act.activation(sq_c[:, :], cg[p][:, s, :], ACT.Square, scale=float(D) ** -0.5, accum_out=cssq[p][:, s:s + 1]).then_inc(cssq_ok, 1)
                b = st.b(1)
                if b.within(B):
                    act.wait_ge(vkv_ps, b.value(plus=1))
                    act.wait_ge(pv_ps, b.value(plus=-1))
                    v = vpad[b.first % 2][:, :, :].rearrange("p (t e) c -> p t e c", e=2)
                    src = ps_prep[:, 0:P].rearrange("p (t e d) -> p t e d", e=2, d=HD)
                    act.activation(v[:, :, 0, 0:HD], src[:, :, 0, :], ACT.Copy)
                    act.activation(v[:, :, 1, HD:2 * HD], src[:, :, 1, :], ACT.Copy).then_inc(v_ok, 1)
                    gb = Count(b.first // GROUP, UNROLL // GROUP, b.it)
                    act.wait_ge(crs_ok, gb.value(plus=1))
                    act.wait_ge(selv_ps, b.value(plus=-3))
                    act.activation(kv1[b.first % 4][:, :], ps_prep[:, P:3 * P], ACT.Copy,
                                   scale=crs[gb.first % 2][:, b.first % GROUP:b.first % GROUP + 1]).then_inc(kv1_ok, 1)
                if g.within(NG):
                    p = g.first % 2
                    if s == 0:
                        act.wait_ge(xT_ps, g.value(plus=1))
                        act.wait_ge(q_ps, g.value())
                        act.activation(xT[:, :], ps_prep[:, :], ACT.Copy).then_inc(xT_ok, 1)
                    elif s == 1:
                        act.wait_ge(q_ps, g.value(plus=1))
                        act.wait_ge(q_written, g.value(96))
                        act.activation(q3[:, 0, :], ps_prep[:, :], ACT.Identity, bias=cols[:, 0:1]).then_inc(q_hi, 1)
                    elif s == 2:
                        act.wait_ge(cT_ps, g.value(plus=1))
                        act.wait_ge(vkv_ps, g.value(GROUP, -GROUP))
                        act.wait_ge(k_ps, g.value(plus=-1))
                        act.activation(cT[p][:, :], ps_prep[:, :], ACT.Copy).then_inc(cT_ok, 1)
                b = st.b(2)
                if b.within(B):
                    act.wait_ge(mT_ps, b.value(plus=1))
                    act.wait_ge(m_stacked, b.value(32))
                    act.activation(m_hi[:, :], ps_a[0][0:H, 0:P], ACT.Copy).then_inc(m_hi_ok, 1)
                b = st.b(-1)
                if b.within(B):
                    act.wait_ge(x1_ok, b.value(plus=1))
                    act.wait_ge(xms_ok, b.value())
                    act.wait_ge(xssq_ok, b.value())
                    act.activation(sq_x[:, :], x1[b.first % 4][:, :], ACT.Square, scale=(float(HD) / D) ** 0.5, accum_out=xssq[:, :]).then_inc(xssq_ok, 1)

            run(act, step)

        @block.vector
        def _(dve):
            dve.wait_ge(cols_in, 16 * 7)
            nc.vector.tensor_copy(bv_rep[:, :], cols[:, 2:3].to_broadcast([P, P])).then_inc(bv_ok, 1)
            dve.wait_ge(rows_in, 16 * 3)
            dve.wait_ge(c0_ps, 1)
            nc.vector.tensor_tensor(c0[:, :], ps_tok[:, 0:P], rows_bc[:, 0, :], ALU.add).then_inc(c0_ok, 1)

            def step(st):
                s = st.s
                ahead = st.b(2)

                def maxima(c):
                    if ahead.within(B):
                        dve.wait_ge(a_ps, ahead.value(4, c + 1))
                        if c == 0:
                            dve.wait_ge(mT_ps, ahead.value())
                        nc.vector.tensor_reduce(negmax[:, 4 * c:4 * c + 4], ps_a[c % 2][:, :].rearrange("p (h k) -> p h k", h=4),
                                                AX.X, ALU.max, negate=True).then_inc(a_max, 1)

                maxima(0)
                maxima(1)
                b = st.b(-1)
                if b.within(B):
                    pair = ps_tok[:, 0:2 * P].rearrange("p (t c) -> p t c", c=32)
                    dve.wait_ge(tok_ps, b.value(plus=1))
                    nc.vector.reciprocal(rden[:, :, :], pair[:, :, 16:32:HD]).then_inc(rden_ok, 1)
                    dve.wait_ge(rden_ok, b.value(plus=1))
                    dve.wait_ge(onT_ps, b.value())
                    nc.vector.tensor_tensor(on[:, :].rearrange("p (t e d) -> p t e d", e=2, d=HD),
                                            pair[:, :, 0:16].rearrange("p t (e d) -> p t e d", d=HD),
                                            rden[:, :, :, None].to_broadcast([P, T, 2, HD]), ALU.mult).then_inc(on_ok, 1)
                maxima(2)
                b = st.b(-2)
                if b.within(B):
                    dve.wait_ge(selk_ps, b.value(plus=1))
                    dve.wait_ge(q1_ok, b.value(plus=1))
                    nc.vector.tensor_tensor(prodk[:, :, :].rearrange("p (j h) d -> p j (h d)", j=3),
                                            ps_sel[:, 0:3 * P].rearrange("p (j n) -> p j n", j=3),
                                            q1[:, None, :].to_broadcast([P, 3, P]), ALU.mult).then_inc(prodk_ok, 1)
                maxima(3)
                if b.within(B):
                    dve.wait_ge(prodk_ok, b.value(plus=1))
                    nc.vector.tensor_reduce(s48[:, :], prodk[:, :, :], AX.X, ALU.add).then_inc(s48_ok, 1)
                a = st.b(-1)
                if a.within(B):
                    dve.wait_ge(wo_ps, a.value(plus=1))
                    dve.wait_ge(xb_ok, a.value(plus=1))
                    nc.vector.tensor_tensor(y[:, :], ps_tok[:, 0:P], xb[a.first % 2][:, :], ALU.add).then_inc(y_ok, 1)
                    dve.wait_ge(y_ok, a.value(plus=1))
                    nc.vector.bn_stats(bn[:, :], y[:, :]).then_inc(bn_ok, 1)
                    dve.wait_ge(bn_ok, a.value(plus=1))
                    dve.wait_ge(ve_ok, a.value())
                if b.within(B):
                    dve.wait_ge(s48_ok, b.value(plus=1))
                    dve.wait_ge(xrs_ok, b.value(plus=1))
                    nc.vector.tensor_scalar(r48[:, :], s48[:, :], 0.0, xrs[b.first % 2][:, :], ALU.max, ALU.mult).then_inc(r48_ok, 1)
                if a.within(B):
                    nc.vector.bn_aggr(mv[:, :], bn[:, :]).then_inc(mv_ok, 1)
                if b.within(B):
                    dve.wait_ge(r48_ok, b.value(plus=1))
                    nc.vector.tensor_tensor(w48[:, :, :].rearrange("p j h -> p (j h)"), r48[:, :], r48[:, :], ALU.mult).then_inc(w48_ok, 1)
                    dve.wait_ge(w48_ok, b.value(plus=1))
                    nc.vector.tensor_reduce(den[:, :], w48[:, :, :].rearrange("p j h -> p h j"), AX.X, ALU.add).then_inc(den_ok, 1)
                    dve.wait_ge(den_ok, b.value(plus=1))
                    nc.vector.tensor_scalar(denm[:, :], den[:, :], DEN_EPS, None, ALU.max).then_inc(denm_ok, 1)
                    dve.wait_ge(denm_ok, b.value(plus=1))
                    nc.vector.reciprocal(rec[:, :], denm[:, :]).then_inc(rec_ok, 1)
                    dve.wait_ge(rec_ok, b.value(plus=1))
                    nc.vector.tensor_tensor(wn[:, :, :], w48[:, :, :], rec[:, None, :].to_broadcast([P, 3, H]), ALU.mult).then_inc(wn_ok, 1)
                    dve.wait_ge(wn_ok, b.value(plus=1))
                    dve.wait_ge(selv_ps, b.value(plus=1))
                    nc.vector.tensor_tensor(prodv[:, :, :].rearrange("p j (h d) -> p (j h) d", d=HD),
                                            ps_sel[:, 0:3 * P].rearrange("p (c d) -> p c d", d=HD),
                                            wn[:, :, :].rearrange("p j h -> p (j h)")[:, :, None].to_broadcast([P, 3 * H, HD]),
                                            ALU.mult).then_inc(prodv_ok, 1)
                    dve.wait_ge(prodv_ok, b.value(plus=1))
                    dve.wait_ge(o1T_ps, b.value())
                    nc.vector.tensor_reduce(o1[:, :], prodv[:, :, :].rearrange("p j n -> p n j"), AX.X, ALU.add).then_inc(o1_ok, 1)
                b = st.b(-3)
                if b.within(B):
                    gb = Count(b.first // GROUP, UNROLL // GROUP, b.it)
                    dve.wait_ge(wo1_ps, b.value(plus=1))
                    if b.first % GROUP == 0:
                        dve.wait_ge(out_stored[gb.first % 2], gb.half().value(16))
                    nc.vector.tensor_tensor(outg[gb.first % 2][:, b.first % GROUP, :], ps_l1[:, 0:P],
                                            x1[b.first % 4][:, :], ALU.add).then_inc(out_ok, 1)
                g = st.g(2)
                if g.within(NG):
                    p = g.first % 2
                    if s == 1:
                        dve.wait_ge(q_hi, g.value(plus=1))
                        dve.wait_ge(q_lo, g.value())
                        nc.vector.scalar_tensor_tensor(out=rq[:, :], in0=ps_prep[:, :], scalar=cols[:, 0:1],
                                                       in1=q3[:, 0, :], op0=ALU.add, op1=ALU.subtract).then_inc(q_r, 1)
                    elif s == 2:
                        dve.wait_ge(mask_in[p], g.half().value(16, 16))
                        nc.vector.tensor_scalar(keep[:, :], maskb[p][:, :], 0.0, None, ALU.not_equal).then_inc(keep_ok, 1)
                        g1 = st.g(1)
                        if g1.first >= 0:
                            dve.wait_ge(k_stacked[g1.first % 2], g1.half().value(32, 32))
                        nc.vector.tensor_scalar(mrow[0:1, :], maskb[p][0:1, :], 0.0, MASKED / SCALE, ALU.is_equal, ALU.mult).then_inc(mrow_ok, 1)
                    elif s == 3:
                        dve.wait_ge(k_ps, g.value(plus=1))
                        dve.wait_ge(keep_ok, g.value(plus=1))
                        dve.wait_ge(k_r, g.value())
                        nc.vector.scalar_tensor_tensor(out=kf[:, :], in0=ps_prep[:, :], scalar=cols[:, 1:2],
                                                       in1=keep[:, :], op0=ALU.add, op1=ALU.mult).then_inc(k_f, 1)
                        dve.wait_ge(k_f, g.value(plus=1))
                        dve.wait_ge(k_written, g.value(96))
                        nc.vector.tensor_copy(k3[:, 0, :], kf[:, :]).then_inc(k_hi, 1)
                if ahead.within(B):
                    dve.wait_ge(m_hi_ok, ahead.value(plus=1))
                    dve.wait_ge(m_stacked, ahead.value(32))
                    nc.vector.tensor_tensor(m_lo[:, :], ps_a[0][0:H, 0:P], m_hi[:, :], ALU.subtract).then_inc(m_lo_ok, 1)
                b = st.b(-1)
                if b.within(B):
                    dve.wait_ge(rstd_ok, b.value(plus=1))
                    dve.wait_ge(t2_ok, b.value())
                    nc.vector.tensor_scalar(t1[:, :], y[:, :], mv[:, 0:1], rstd[:, :], ALU.subtract, ALU.mult).then_inc(t1_ok, 1)

            run(dve, step)


_INS = ['x', 'ctx_1024', 'itok_BxS_0_255', 'mask_BxS2_if1', 'L0_xattn_Wq', 'L0_xattn_bq', 'L0_xattn_Wk', 'L0_xattn_bk',
        'L0_xattn_Wv', 'L0_xattn_bv', 'L0_xattn_Wo', 'L0_xattn_bo', 'L0_xattn_ln_gamma', 'L0_xattn_ln_beta',
        'L1_xattn_gamma_q', 'L1_xattn_gamma_kv', 'L1_xattn_Wq', 'L1_xattn_Wk', 'L1_xattn_Wv', 'L1_xattn_Wo']


def kernel(**inputs):
    import numpy as _np
    import concourse.bacc as _bacc
    from concourse import mybir as _mybir
    from concourse.bass_utils import run_bass_kernel_spmd as _run

    nc = _bacc.Bacc("TRN2", target_bir_lowering=False, num_devices=1)
    arrays, args = {}, []
    for name in _INS:
        a = _np.ascontiguousarray(inputs[name])
        arrays[f"in_{name}_dram"] = a
        args.append(nc.dram_tensor(f"in_{name}_dram", a.shape, _mybir.dt.from_np(a.dtype), kind="ExternalInput").ap())
    shape = inputs['x'].shape
    args.append(nc.dram_tensor("out_0_dram", shape, _mybir.dt.float32, kind="ExternalOutput").ap())
    xattn_kernel(nc, *args)
    r = _run(nc, [arrays], core_ids=[0])
    return r.results[0]["out_0_dram"]
```

```python
from contextlib import ExitStack

import concourse.bass as bass
from concourse import mybir

ALU = mybir.AluOpType
ACT = mybir.ActivationFunctionType
AX = mybir.AxisListType
F32 = mybir.dt.float32
BF16 = mybir.dt.bfloat16
I32 = mybir.dt.int32

LN_EPS = 1e-5
RMS_EPS = 1.1920929e-07
DEN_EPS = 1e-6
MASKED = -1e9

GROUP = 4
UNROLL = 2 * GROUP
TERMS = 6
Q_RUNS = ((0, 3), (3, 2), (5, 1))
K_RUNS = ((0, 3), (3, 2), (5, 1))


class Step:

    def __init__(self, base, it=None):
        self.base, self.it = base, it
        self.s = base % GROUP

    def b(self, lag):
        return Count(self.base + lag, UNROLL, self.it)

    def g(self, lag):
        return Count(self.base // GROUP + lag, UNROLL // GROUP, self.it)


class Count:

    def __init__(self, first, stride, it):
        self.first, self.stride, self.it = first, stride, it

    def within(self, n):
        return 0 <= self.first < n

    def value(self, times=1, plus=0):
        v = self.first * times + plus
        if self.it is None:
            return max(v, 0)
        assert v > 0
        return v + self.it * (self.stride * times)

    def half(self):
        return Count(self.first // 2, self.stride // 2, self.it)


def xattn_kernel(nc, x, xT_in, ctx, cT_in, idx, mask, w_qk, w_rest, cols_in, rows_in, out):
    B, S, D = x.shape
    H = 16
    HD = D // H
    T = H // 2
    NG = B // GROUP
    GT = GROUP * S
    E_ROWS = TERMS * HD
    MASK_ROW = 2 * E_ROWS
    M_ROW = MASK_ROW + 1
    A_ROWS = MASK_ROW + 1
    B_ROWS = M_ROW + 2
    CH = 4
    SCALE = float(HD) ** -0.5
    FLOOR_SCALE = DEN_EPS * HD
    SETUP_OPS = 13
    P = 128
    assert S == P and D == P and NG >= 8 and NG % 2 == 0

    es = ExitStack()
    with es:
        def sb(name, shape, dt=F32):
            return es.enter_context(nc.sbuf_tensor(name, shape, dt))

        def sem(name):
            return es.enter_context(nc.semaphore(name))

        def sems(name, n):
            return [sem(f"{name}{i}") for i in range(n)]

        q_scr = [nc.dram_tensor(f"q_scr{i}", [TERMS, D, GT], BF16).ap() for i in range(2)]
        k_scr = [nc.dram_tensor(f"k_scr{i}", [TERMS, D, GT], BF16).ap() for i in range(2)]

        ident = sb("ident", [P, P])
        wqk = sb("wqk", [P, 2, P])
        wrest = sb("wrest", [P, 6, P])
        woT, wq1T, wo1T = wrest[:, 3, :], wrest[:, 4, :], wrest[:, 5, :]
        cols = sb("cols", [P, 5])
        rows_bc = sb("rows_bc", [P, 3, P])
        ones = sb("ones", [2, GT], BF16)
        bv_rep = sb("bv_rep", [P, P])
        c0 = sb("c0", [P, P])
        pos = sb("pos", [P, 3])
        m_half = sb("m_half", [P, GROUP])
        eps = sb("eps", [P, GROUP + 2])

        xT = [sb(f"xT{i}", [P, GT]) for i in range(2)]
        cTk = [sb(f"cTk{i}", [P, GT]) for i in range(2)]
        cTv = [sb(f"cTv{i}", [P, GT]) for i in range(2)]
        cg = [sb(f"cg{i}", [P, GROUP, P]) for i in range(2)]
        xres = [sb(f"xres{i}", [P, GROUP, P]) for i in range(2)]
        maskb = [sb(f"maskb{i}", [P, GT], I32) for i in range(2)]
        idxb = [sb(f"idxb{i}", [P, GT], I32) for i in range(2)]
        onehot = [sb(f"onehot{i}", [P, 3, GT]) for i in range(2)]
        keep = sb("keep", [P, GT])
        mrow = sb("mrow", [1, GT], BF16)
        q3 = sb("q3", [P, 3, GT], BF16)
        k3 = sb("k3", [P, 3, GT], BF16)
        rq = sb("rq", [P, GT])
        kf = sb("kf", [P, GT])
        rk = sb("rk", [P, GT])
        qst = [sb(f"qst{i}", [P, T, 2, GT], BF16) for i in range(2)]
        kst = [sb(f"kst{i}", [P, T, GT], BF16) for i in range(2)]
        cssq = [sb(f"cssq{i}", [P, GROUP]) for i in range(2)]
        cms = sb("cms", [P, GROUP])
        crs = [sb(f"crs{i}", [P, GROUP]) for i in range(2)]
        outg = [sb(f"outg{i}", [P, GROUP, P]) for i in range(2)]

        vpad = [sb(f"vpad{i}", [P, H, 32]) for i in range(2)]
        kv1 = [sb(f"kv1_{i}", [P, 2 * P]) for i in range(4)]
        negmax = sb("negmax", [P, H])
        m_hi = sb("m_hi", [H, P], BF16)
        m_lo = sb("m_lo", [H, P], BF16)
        probs = [sb(f"probs{i}", [P, CH, 4 * P]) for i in range(2)]
        pvs = sb("pvs", [P, 2, P])
        rden = sb("rden", [P, T, 2])
        on = sb("on", [P, P])
        onT = sb("onT", [P, P])
        xb = [sb(f"xb{i}", [P, P]) for i in range(2)]
        y = sb("y", [P, P])
        bn = sb("bn", [P, 6])
        mv = sb("mv", [P, 2])
        ve = sb("ve", [P, 1])
        rstd = sb("rstd", [P, 1])
        t1 = sb("t1", [P, P])
        t2 = sb("t2", [P, P])
        x1 = [sb(f"x1_{i}", [P, P]) for i in range(4)]
        sq_c = sb("sq_c", [P, P])
        sq_x = sb("sq_x", [P, P])
        xssq = sb("xssq", [P, 1])
        floor = sb("floor", [P, 1])
        x1T = sb("x1T", [P, P])
        q1 = sb("q1", [P, P])
        prodk = sb("prodk", [P, 3 * H, HD])
        s48 = sb("s48", [P, 3 * H])
        w48 = sb("w48", [P, 3, H])
        den = sb("den", [P, H])
        denm = sb("denm", [P, H])
        rec = sb("rec", [P, H])
        wn = sb("wn", [P, 3, H])
        prodv = sb("prodv", [P, 3, P])
        o1a = sb("o1a", [P, P])
        o1 = sb("o1", [P, P])
        o1T = sb("o1T", [P, P])

        def bank(name):
            return es.enter_context(nc.psum_tensor(name, [P, 512], F32))

        ps_a = [bank("ps_a0"), bank("ps_a1")]
        ps_b = [bank("ps_b0"), bank("ps_b1")]
        ps_tok = bank("ps_tok")
        ps_prep = bank("ps_prep")
        ps_l1 = bank("ps_l1")
        ps_sel = bank("ps_sel")

        wqk_in, wrest_in, vec_in, ones_in = sem("wqk_in"), sem("wrest_in"), sem("vec_in"), sem("ones_in")
        pool_setup, ones_ok, qst_zero, vpad_ok = sem("pool_setup"), sem("ones_ok"), sem("qst_zero"), sem("vpad_ok")
        wt_ok, bv_ok, c0_ps, c0_ok = sem("wt_ok"), sem("bv_ok"), sem("c0_ps"), sem("c0_ok")
        x_in, ck_in, cv_in, c_in, mask_in = [sems(n, 2) for n in ("x_in", "ck_in", "cv_in", "c_in", "mask_in")]
        idx_in, xres_in = sems("idx_in", 2), sems("xres_in", 2)
        q_ps, q_hi, q_r, q_mid, q_lo = [sem(n) for n in ("q_ps", "q_hi", "q_r", "q_mid", "q_lo")]
        k_ps, k_f, k_hi, k_r, k_mid, k_lo = [sem(n) for n in ("k_ps", "k_f", "k_hi", "k_r", "k_mid", "k_lo")]
        keep_ok, mrow_ok = sem("keep_ok"), sem("mrow_ok")
        q_written, k_written = sem("q_written"), sem("k_written")
        q_stacked, k_stacked = sems("q_stacked", 2), sems("k_stacked", 2)
        cssq_ok, cms_ok, crs_ok = sem("cssq_ok"), sem("cms_ok"), sem("crs_ok")
        onehot_ok, onehot2_ok = sem("onehot_ok"), sem("onehot2_ok")
        vkv_ps, v_ok, kv1_ok = sem("vkv_ps"), sem("v_ok"), sem("kv1_ok")
        a_ps, a_max, mT_ps, m_hi_ok, m_lo_ok, m_stacked = [sem(n) for n in ("a_ps", "a_max", "mT_ps", "m_hi_ok", "m_lo_ok", "m_stacked")]
        b_ps, exp_ok, pv_ps, pvs_ok = sem("b_ps"), sem("exp_ok"), sem("pv_ps"), sem("pvs_ok")
        tok_ps, rden_ok, on_ok, onT_ps, onT_ok, wo_ps = [sem(n) for n in ("tok_ps", "rden_ok", "on_ok", "onT_ps", "onT_ok", "wo_ps")]
        xb_ok, y_ok, bn_ok, mv_ok, ve_ok, rstd_ok, t1_ok, t2_ok, x1_ok = [sem(n) for n in (
            "xb_ok", "y_ok", "bn_ok", "mv_ok", "ve_ok", "rstd_ok", "t1_ok", "t2_ok", "x1_ok")]
        xssq_ok, floor_ok, o1a_ok = sem("xssq_ok"), sem("floor_ok"), sem("o1a_ok")
        x1T_ps, x1T_ok, q1_ps, q1_ok = sem("x1T_ps"), sem("x1T_ok"), sem("q1_ps"), sem("q1_ok")
        selk_ps, prodk_ok, s48_ok, w48_ok, den_ok, denm_ok, rec_ok, wn_ok = [sem(n) for n in (
            "selk_ps", "prodk_ok", "s48_ok", "w48_ok", "den_ok", "denm_ok", "rec_ok", "wn_ok")]
        selv_ps, prodv_ok, o1_ok, o1T_ps, o1T_ok, wo1_ps, out_ok = [sem(n) for n in (
            "selv_ps", "prodv_ok", "o1_ok", "o1T_ps", "o1T_ok", "wo1_ps", "out_ok")]
        out_stored = sems("out_stored", 2)

        FIRST, LOOP, LAST = -2 * GROUP, UNROLL, B + GROUP
        LOOPS = (B - 2 * GROUP - LOOP) // UNROLL

        def run(eng, step):
            for n in range(FIRST, LOOP):
                step(Step(n))
            with eng.Fori(0, LOOPS) as it:
                for s in range(UNROLL):
                    step(Step(LOOP + s, it))
            for n in range(LOOP + LOOPS * UNROLL, LAST):
                step(Step(n))

        def rows_of(tensor, g):
            at = g.value(GROUP)
            part = tensor[at:at + GROUP] if g.it is None else tensor[bass.ds(at, GROUP)]
            return part.rearrange("b s d -> s b d")

        def columns_of(tensor, g):
            at = g.value(GT)
            return tensor[:, at:at + GT] if g.it is None else tensor[:, bass.ds(at, GT)]

        def bcast_of(tensor, g):
            at = g.value(GT)
            flat = tensor.rearrange("(a b) s -> a (b s)", a=1)
            part = flat[:, at:at + GT] if g.it is None else flat[:, bass.ds(at, GT)]
            return part.to_broadcast([P, GT])

        block = es.enter_context(nc.Block())

        @block.sync
        def _(sp):
            sp.dma_start(wqk[:, :, :], w_qk).then_inc(wqk_in, 16)

            def write_scratch(scr, parts, runs, repeat, done):
                for i, (t0, n) in enumerate(runs):
                    src = parts[:, i:i + 1, :].to_broadcast([P, n, GT]) if repeat else parts[:, 0:n, :]
                    sp.dma_start(scr[t0:t0 + n].rearrange("t r n -> r t n"), src).then_inc(done, 16)

            def head_rows(scr, e):
                return scr[:, HD * T * e:HD * T * (e + 1), :].rearrange("t (d a) n -> t d (a n)", a=T)

            def load_group(g, p):
                sp.dma_start(xT[p][:, :], columns_of(xT_in, g)).then_inc(x_in[p], 16)
                sp.dma_start(cTk[p][:, :], columns_of(cT_in, g)).then_inc(ck_in[p], 16)
                sp.dma_start(maskb[p][:, :], bcast_of(mask, g)).then_inc(mask_in[p], 16)

            def load_context(g, p):
                sp.dma_start(cg[p][:, :, :], rows_of(ctx, g)).then_inc(c_in[p], 16)

            def step(st):
                s = st.s
                if st.it is None and st.base == FIRST:
                    for g in range(2):
                        load_group(Count(g, 0, None), g)
                    sp.dma_start(wrest[:, :, :], w_rest).then_inc(wrest_in, 16)
                    for g in range(2):
                        load_context(Count(g, 0, None), g)
                g = st.g(2)
                if s == 0 and g.first >= 2 and g.within(NG):
                    load_group(g, g.first % 2)
                b, g = st.b(1), st.g(1)
                if b.within(B):
                    qs = qst[(b.first // GROUP) % 2]
                    at = (b.first % GROUP) * S
                    for i, (m, ok) in enumerate(((m_hi, m_hi_ok), (m_lo, m_lo_ok))):
                        if i == 1 and s == 0 and g.within(NG):
                            sp.wait_ge(q_written, g.value(48, 48))
                        sp.wait_ge(ok, b.value(plus=1))
                        sp.dma_start(qs[M_ROW + i:M_ROW + i + 1, :, :, at:at + S].rearrange("p t e n -> p (t e) n"),
                                     m[:, :]).then_inc(m_stacked, 16)
                p = g.first % 2
                if s == 0 and g.within(NG):
                    if not b.within(B):
                        sp.wait_ge(q_written, g.value(48, 48))
                    if st.it is None:
                        sp.wait_ge(qst_zero, 2)
                    sp.wait_ge(b_ps, g.value(4 * GROUP, -4 * GROUP))
                    for e in range(2):
                        sp.dma_start(qst[p][E_ROWS * e:E_ROWS * (e + 1), :, e, :],
                                     head_rows(q_scr[p], e)).then_inc(q_stacked[p], 16)
                    sp.wait_ge(k_written, g.value(48, 48))
                    for e in range(2):
                        sp.dma_start(kst[p][E_ROWS * e:E_ROWS * (e + 1), :, :].rearrange("p t n -> p (t n)"),
                                     head_rows(k_scr[p], e)).then_inc(k_stacked[p], 16)
                    sp.wait_ge(mrow_ok, g.value(plus=1))
                    sp.dma_start(kst[p][MASK_ROW:MASK_ROW + 1, :, :],
                                 mrow[0:1, None, :].to_broadcast([1, T, GT])).then_inc(k_stacked[p], 16)
                    if g.first >= 2 or g.it is not None:
                        sp.wait_ge(vkv_ps, g.value(GROUP, -GROUP))
                    sp.dma_start(cTv[p][:, :], columns_of(cT_in, g)).then_inc(cv_in[p], 16)
                g = st.g(2)
                if s == 0 and g.first >= 2 and g.within(NG):
                    load_context(g, g.first % 2)
                p = g.first % 2
                if s == 1 and g.within(NG):
                    sp.wait_ge(q_lo, g.value(plus=1))
                    write_scratch(q_scr[p], q3, Q_RUNS, True, q_written)
                if s == 2 and g.within(NG):
                    sp.wait_ge(k_lo, g.value(plus=1))
                    write_scratch(k_scr[p], k3, K_RUNS, False, k_written)
                if s == 3 and g.within(NG):
                    sp.wait_ge(onehot2_ok, g.value(plus=-1))
                    sp.wait_ge(onehot_ok, g.value(plus=-1))
                    sp.dma_start(idxb[p][:, :], bcast_of(idx, g)).then_inc(idx_in[p], 16)
                g = st.g(1)
                if s == 2 and g.within(NG):
                    sp.wait_ge(xb_ok, g.value(GROUP, -GROUP))
                    sp.dma_start(xres[g.first % 2][:, :, :], rows_of(x, g)).then_inc(xres_in[g.first % 2], 16)
                g = st.g(-1)
                if s == 3 and g.within(NG):
                    sp.wait_ge(out_ok, g.value(GROUP, GROUP))
                    sp.dma_start(rows_of(out, g), outg[g.first % 2][:, :, :]).then_inc(out_stored[g.first % 2], 16)

            run(sp, step)
            for p in range(2):
                sp.wait_ge(out_stored[p], 16 * (NG // 2))

        @block.gpsimd
        def _(pool):
            setup = [0]

            def alone(ins):
                ins.then_inc(pool_setup, 1)
                setup[0] += 1
                pool.wait_ge(pool_setup, setup[0])

            pool.memset(ones[:, :], 1.0).then_inc(ones_ok, 1)
            pool.memset(qst[1][0:2 * E_ROWS, :, :, :].rearrange("p t e n -> p (t e n)").bitcast(F32), 0.0).then_inc(qst_zero, 1)
            alone(pool.memset(ident[:, :], 0.0))
            alone(pool.affine_select(out=ident[:, :], in_=ident[:, :], compare_op=ALU.not_equal, fill=1.0,
                                     base=0, pattern=[[-1, P]], channel_multiplier=1))
            alone(pool.iota(pos[:, :], pattern=[[-1, 3]], base=1, channel_multiplier=1,
                            allow_small_or_imprecise_dtypes=True))
            alone(pool.memset(eps[:, 0:GROUP], RMS_EPS))
            alone(pool.memset(eps[:, GROUP:GROUP + 1], FLOOR_SCALE * RMS_EPS))
            alone(pool.memset(eps[:, GROUP + 1:GROUP + 2], LN_EPS))
            alone(pool.memset(m_half[:, :], -0.5))
            for i in range(2):
                alone(pool.memset(vpad[i][:, :, :], 0.0))
                for e in range(2):
                    v = vpad[i][:, :, :].rearrange("p (t e) c -> p t e c", e=2)
                    alone(pool.memset(v[:, :, e, 16 + HD * e:16 + HD * (e + 1)], 1.0))
            pool.sem_inc(vpad_ok, 1)

            def power(dst, base, n, ok):
                return pool.tensor_tensor(dst, base, m_half[:, 0:n], ALU.pow).then_inc(ok, 1)

            def step(st):
                s = st.s
                b = st.b(-2)
                if b.within(B):
                    pool.wait_ge(t1_ok, b.value(plus=1))
                    pool.tensor_tensor(t2[:, :], t1[:, :], rows_bc[:, 1, :], ALU.mult).then_inc(t2_ok, 1)
                    pool.wait_ge(t2_ok, b.value(plus=1))
                    pool.wait_ge(out_ok, b.value(plus=-3))
                    pool.tensor_tensor(x1[b.first % 4][:, :], t2[:, :], rows_bc[:, 2, :], ALU.add).then_inc(x1_ok, 1)
                b = st.b(-3)
                if b.within(B):
                    pool.wait_ge(prodv_ok, b.value(plus=1))
                    pool.tensor_tensor(o1a[:, :], prodv[:, 0, :], prodv[:, 1, :], ALU.add).then_inc(o1a_ok, 1)
                    pool.wait_ge(o1a_ok, b.value(plus=1))
                    pool.wait_ge(o1T_ps, b.value())
                    pool.tensor_tensor(o1[:, :], o1a[:, :], prodv[:, 2, :], ALU.add).then_inc(o1_ok, 1)
                hot_g = st.g(1) if s == 3 else st.g(0)
                hot = s in (3, 0) and hot_g.within(NG)
                if s == 3 and hot:
                    pool.wait_ge(idx_in[hot_g.first % 2], hot_g.half().value(16, 16))
                    pool.wait_ge(selv_ps, hot_g.value(GROUP, -GROUP))
                b = st.b(0)
                if b.within(B):
                    g = st.g(0)
                    if s == 0:
                        pool.wait_ge(xres_in[g.first % 2], g.half().value(16, 16))
                    if b.first == 0:
                        pool.wait_ge(c0_ok, 1)
                    pool.wait_ge(y_ok, b.value(plus=-1))
                    pool.tensor_tensor(xb[b.first % 2][:, :], xres[g.first % 2][:, s, :], c0[:, :], ALU.add).then_inc(xb_ok, 1)
                if hot:
                    p, j = hot_g.first % 2, (0 if s == 3 else 1)
                    hot_j = pool.tensor_scalar(onehot[p][:, j, :], idxb[p][:, :], pos[:, j:j + 1], None, ALU.is_equal)
                    if j == 1:
                        hot_j.then_inc(onehot_ok, 1)
                g = st.g(1)
                p = g.first % 2
                if s == 0 and g.within(NG):
                    pool.wait_ge(cssq_ok, g.value(GROUP, GROUP))
                    pool.tensor_tensor(cms[:, :], cssq[p][:, :], eps[:, 0:GROUP], ALU.add).then_inc(cms_ok, 1)
                    pool.wait_ge(cms_ok, g.value(plus=1))
                    pool.wait_ge(kv1_ok, g.value(GROUP, -GROUP))
                    power(crs[p][:, :], cms[:, :], GROUP, crs_ok)
                g = st.g(2)
                if s == 1 and g.within(NG):
                    pool.wait_ge(q_mid, g.value(plus=1))
                    pool.tensor_tensor(q3[:, 2, :], rq[:, :], q3[:, 1, :], ALU.subtract).then_inc(q_lo, 1)
                if s == 2 and g.within(NG):
                    pool.wait_ge(k_hi, g.value(plus=1))
                    pool.wait_ge(k_mid, g.value())
                    pool.tensor_tensor(rk[:, :], kf[:, :], k3[:, 0, :], ALU.subtract).then_inc(k_r, 1)
                b = st.b(-2)
                if b.within(B):
                    pool.wait_ge(xssq_ok, b.value(plus=1))
                    pool.wait_ge(denm_ok, b.value())
                    pool.tensor_tensor(floor[:, :], xssq[:, :], eps[:, GROUP:GROUP + 1], ALU.add).then_inc(floor_ok, 1)
                b = st.b(-1)
                if b.within(B):
                    pool.wait_ge(mv_ok, b.value(plus=1))
                    pool.tensor_tensor(ve[:, :], mv[:, 1:2], eps[:, GROUP + 1:GROUP + 2], ALU.add).then_inc(ve_ok, 1)
                if b.within(B):
                    pool.wait_ge(ve_ok, b.value(plus=1))
                    pool.wait_ge(t1_ok, b.value())
                    power(rstd[:, :], ve[:, :], 1, rstd_ok)
                g = st.g(2)
                if s == 2 and g.within(NG):
                    pool.wait_ge(k_mid, g.value(plus=1))
                    pool.tensor_tensor(k3[:, 2, :], rk[:, :], k3[:, 1, :], ALU.subtract).then_inc(k_lo, 1)

            run(pool, step)

        @block.tensor
        def _(pe):
            pe.wait_ge(wqk_in, 16)

            def step(st):
                s = st.s
                cur, ahead, after = st.b(0), st.b(2), st.b(-1)

                def scores_kq(c):
                    if not cur.within(B):
                        return
                    p, at = (cur.first // GROUP) % 2, s * S
                    if c == 0:
                        pe.wait_ge(m_stacked, cur.value(32, 32))
                    pe.wait_ge(exp_ok, cur.value(4, c - 1))
                    for i in range(2):
                        t = 2 * c + i
                        last = nc.tensor.matmul(ps_b[c % 2][:, 2 * P * i:2 * P * (i + 1)],
                                                kst[p][0:B_ROWS, t, at:at + S],
                                                qst[p][0:B_ROWS, t, :, at:at + S], start=True, stop=True)
                    last.then_inc(b_ps, 1)

                def scores_qk(c):
                    if not ahead.within(B):
                        return
                    p, at = (ahead.first // GROUP) % 2, (ahead.first % GROUP) * S
                    if c == 0 and ahead.it is None and ahead.first == 0:
                        pe.wait_ge(ones_in, 16 * 4)
                        pe.wait_ge(pool_setup, SETUP_OPS)
                        pe.wait_ge(wt_ok, 1)
                    if c == 0 and at == 0:
                        gh = st.g(1).half()
                        pe.wait_ge(q_stacked[p], gh.value(32, 32))
                        pe.wait_ge(k_stacked[p], gh.value(48, 48))
                    if c == 0:
                        pe.wait_ge(m_hi_ok, ahead.value())
                        pe.wait_ge(m_lo_ok, ahead.value())
                    else:
                        pe.wait_ge(a_max, ahead.value(4, 0 if c == 1 else c - 1))
                    for h in range(4 * c, 4 * c + 4):
                        t, e = h // 2, h % 2
                        last = nc.tensor.matmul(ps_a[c % 2][:, (h % 4) * P:(h % 4 + 1) * P],
                                                qst[p][0:A_ROWS, t, e, at:at + S],
                                                kst[p][0:A_ROWS, t, at:at + S], start=True, stop=True)
                    last.then_inc(a_ps, 1)

                def max_rows():
                    if ahead.within(B):
                        pe.wait_ge(a_max, ahead.value(4, 4))
                        nc.tensor.matmul(ps_a[0][0:H, 0:P], negmax[:, :], ident[:, :], start=True, stop=True).then_inc(mT_ps, 1)

                def values():
                    if not cur.within(B):
                        return
                    pe.wait_ge(v_ok, cur.value(plus=1))
                    if cur.it is None and cur.first == 0:
                        pe.wait_ge(c0_ok, 1)
                    pe.wait_ge(y_ok, cur.value())
                    for half in range(2):
                        pe.wait_ge(exp_ok, cur.value(4, 2 * half + 2))
                        for e in range(2):
                            for j in range(4):
                                h = 8 * half + 2 * j + e
                                last = nc.tensor.matmul(ps_tok[32 * j:32 * j + 32, P * half:P * (half + 1)],
                                                        vpad[cur.first % 2][:, h, :],
                                                        probs[cur.first % 2][:, h // 4, (h % 4) * P:(h % 4 + 1) * P],
                                                        start=(e == 0), stop=(e == 1))
                    last.then_inc(pv_ps, 1)

                def to_tokens():
                    if after.within(B):
                        pe.wait_ge(pvs_ok, after.value(plus=1))
                        for half in range(2):
                            last = nc.tensor.transpose(ps_tok[:, P * half:P * (half + 1)], pvs[:, half, :], ident[:, :])
                        last.then_inc(tok_ps, 1)

                def to_features():
                    if after.within(B):
                        pe.wait_ge(on_ok, after.value(plus=1))
                        nc.tensor.transpose(ps_tok[:, 0:P], on[:, :], ident[:, :]).then_inc(onT_ps, 1)

                def out_proj0():
                    if after.within(B):
                        pe.wait_ge(onT_ok, after.value(plus=1))
                        nc.tensor.matmul(ps_tok[:, 0:P], onT[:, :], woT, start=True, stop=True).then_inc(wo_ps, 1)

                def l1_transpose():
                    b = st.b(-2)
                    if b.within(B):
                        pe.wait_ge(x1_ok, b.value(plus=1))
                        pe.wait_ge(prodv_ok, b.value())
                        nc.tensor.transpose(ps_sel[:, 3 * P:4 * P], x1[b.first % 4][:, :], ident[:, :]).then_inc(x1T_ps, 1)

                def l1_query():
                    b = st.b(-2)
                    if b.within(B):
                        pe.wait_ge(x1T_ok, b.value(plus=1))
                        pe.wait_ge(out_ok, b.value(plus=-1))
                        nc.tensor.matmul(ps_l1[:, 0:P], x1T[:, :], wq1T, start=True, stop=True).then_inc(q1_ps, 1)

                def select(which, done):
                    b = st.b(-2)
                    if not b.within(B):
                        return
                    i = b.first % GROUP
                    if which == 0:
                        if i == 0:
                            pe.wait_ge(onehot_ok, st.g(0).value(plus=1))
                            pe.wait_ge(onehot2_ok, st.g(0).value(plus=1))
                        pe.wait_ge(kv1_ok, b.value(plus=1))
                    else:
                        pe.wait_ge(prodk_ok, b.value(plus=1))
                    for j in range(3):
                        last = nc.tensor.matmul(ps_sel[:, P * j:P * (j + 1)],
                                                onehot[(b.first // GROUP) % 2][:, j, i * S:(i + 1) * S],
                                                kv1[b.first % 4][:, P * which:P * (which + 1)], start=True, stop=True)
                    last.then_inc(done, 1)

                def l1_out_transpose():
                    b = st.b(-3)
                    if b.within(B):
                        pe.wait_ge(o1_ok, b.value(plus=1))
                        if st.b(-2).within(B):
                            pe.wait_ge(q1_ok, st.b(-2).value(plus=1))
                        else:
                            pe.wait_ge(out_ok, b.value())
                        nc.tensor.transpose(ps_l1[:, 0:P], o1[:, :], ident[:, :]).then_inc(o1T_ps, 1)

                def l1_out_proj():
                    b = st.b(-3)
                    if b.within(B):
                        pe.wait_ge(o1T_ok, b.value(plus=1))
                        nc.tensor.matmul(ps_l1[:, 0:P], o1T[:, :], wo1T, start=True, stop=True).then_inc(wo1_ps, 1)

                def project_ctx():
                    b = st.b(1)
                    if not b.within(B):
                        return
                    i, p = b.first % GROUP, (b.first // GROUP) % 2
                    gb = Step(st.base - 1, st.it).g(2)
                    if s == 1 and gb.within(NG):
                        pe.wait_ge(q_r, gb.value(plus=1))
                    elif s == 2 and gb.within(NG):
                        pe.wait_ge(k_f, gb.value(plus=1))
                    else:
                        pe.wait_ge(kv1_ok, b.value())
                    if i == 0:
                        gh = Count(b.first // GROUP, UNROLL // GROUP, b.it).half()
                        pe.wait_ge(cv_in[p], gh.value(16, 16))
                    nc.tensor.matmul(ps_prep[:, 0:3 * P], cTv[p][:, i * S:(i + 1) * S],
                                     wrest[:, 0:3, :], start=True, stop=True).then_inc(vkv_ps, 1)

                def group_piece():
                    g = st.g(2)
                    if s > 1 or not g.within(NG):
                        return
                    p = g.first % 2
                    if st.b(1).within(B):
                        pe.wait_ge(kv1_ok, st.b(1).value(plus=1))
                    if s == 0:
                        pe.wait_ge(x_in[p], g.half().value(16, 16))
                        pe.wait_ge(k_f, g.value())
                        nc.tensor.matmul(ps_prep[:, :], wqk[:, 0, :], xT[p][:, :], start=True, stop=True).then_inc(q_ps, 1)
                    else:
                        pe.wait_ge(ck_in[p], g.half().value(16, 16))
                        pe.wait_ge(q_r, g.value(plus=1))
                        nc.tensor.matmul(ps_prep[:, :], wqk[:, 1, :], cTk[p][:, :], start=True, stop=True).then_inc(k_ps, 1)

                if st.it is None and st.base == -1:
                    pe.wait_ge(bv_ok, 1)
                    nc.tensor.matmul(ps_tok[:, 0:P], bv_rep[:, :], woT, start=True, stop=True).then_inc(c0_ps, 1)
                scores_kq(0)
                scores_qk(0)
                scores_kq(1)
                to_tokens()
                scores_qk(1)
                l1_transpose()
                scores_kq(2)
                scores_qk(2)
                project_ctx()
                to_features()
                l1_query()
                scores_kq(3)
                scores_qk(3)
                out_proj0()
                l1_out_transpose()
                select(0, selk_ps)
                l1_out_proj()
                max_rows()
                values()
                group_piece()
                select(1, selv_ps)

            run(pe, step)

        @block.scalar
        def _(act):
            with nc.allow_non_contiguous_dma("five numbers a partition, once"):
                act.dma_start(cols[:, :], cols_in).then_inc(vec_in, 16)
            act.dma_start(rows_bc[:, :, :].rearrange("p a n -> p (a n)"),
                          rows_in.rearrange("(b a) n -> b (a n)", b=1).to_broadcast([P, 3 * P])).then_inc(vec_in, 16)
            act.wait_ge(ones_ok, 1)
            for i in range(2):
                act.dma_start(qst[i][MASK_ROW:MASK_ROW + 1, :, :, :].rearrange("p t e n -> p (t e) n"),
                              ones[0:1, None, :].to_broadcast([1, 2 * T, GT])).then_inc(ones_in, 16)
                act.dma_start(kst[i][M_ROW:M_ROW + 2, :, :],
                              ones[0:2, None, :].to_broadcast([2, T, GT])).then_inc(ones_in, 16)
            act.wait_ge(vec_in, 32)

            def scale_weights():
                act.wait_ge(wrest_in, 16)
                kv = wrest[:, 1:3, :].rearrange("p a n -> p (a n)")
                act.activation(kv, kv, ACT.Copy, scale=cols[:, 4:5])
                act.activation(wq1T, wq1T, ACT.Copy, scale=cols[:, 3:4]).then_inc(wt_ok, 1)

            def step(st):
                s = st.s
                cur = st.b(0)
                g2 = st.g(2)

                def exps(c):
                    if cur.within(B):
                        act.wait_ge(b_ps, cur.value(4, c + 1))
                        if c == 0:
                            act.wait_ge(pv_ps, cur.value(plus=-1))
                        act.activation(probs[cur.first % 2][:, c, :], ps_b[c % 2][:, :], ACT.Exp, scale=SCALE).then_inc(exp_ok, 1)

                if st.it is None and st.base == FIRST + 3:
                    scale_weights()
                exps(0)
                if s == 1 and g2.within(NG):
                    act.wait_ge(q_r, g2.value(plus=1))
                    act.activation(q3[:, 1, :], rq[:, :], ACT.Copy).then_inc(q_mid, 1)
                if s == 2 and g2.within(NG):
                    act.wait_ge(k_f, g2.value(plus=1))
                    act.wait_ge(k_written, g2.value(48))
                    act.activation(k3[:, 0, :], kf[:, :], ACT.Copy).then_inc(k_hi, 1)
                exps(1)
                b = st.b(2 * GROUP - 1)
                if b.within(B):
                    gb = Count(b.first // GROUP, UNROLL // GROUP, b.it)
                    p, i = gb.first % 2, b.first % GROUP
                    if i == 0:
                        act.wait_ge(c_in[p], gb.half().value(16, 16))
                        act.wait_ge(cms_ok, gb.value(plus=-1))
                    act.wait_ge(cssq_ok, b.value())
                    act.activation(sq_c[:, :], cg[p][:, i, :], ACT.Square, scale=float(D) ** -0.5, accum_out=cssq[p][:, i:i + 1]).then_inc(cssq_ok, 1)
                b = st.b(-2)
                if b.within(B):
                    act.wait_ge(x1T_ps, b.value(plus=1))
                    act.wait_ge(q1_ps, b.value())
                    act.activation(x1T[:, :], ps_sel[:, 3 * P:4 * P], ACT.Copy).then_inc(x1T_ok, 1)
                    act.wait_ge(x1_ok, b.value(plus=1))
                    act.wait_ge(floor_ok, b.value())
                    act.wait_ge(xssq_ok, b.value())
                    act.activation(sq_x[:, :], x1[b.first % 4][:, :], ACT.Square, scale=(FLOOR_SCALE / D) ** 0.5, accum_out=xssq[:, :]).then_inc(xssq_ok, 1)
                exps(2)
                b = st.b(1)
                if b.within(B):
                    if b.it is None and b.first == 0:
                        act.wait_ge(vpad_ok, 1)
                    act.wait_ge(vkv_ps, b.value(plus=1))
                    act.wait_ge(pv_ps, b.value(plus=-1))
                    v = vpad[b.first % 2][:, :, :].rearrange("p (t e) c -> p t e c", e=2)
                    src = ps_prep[:, 0:P].rearrange("p (t e d) -> p t e d", e=2, d=HD)
                    act.activation(v[:, :, 0, 0:HD], src[:, :, 0, :], ACT.Copy)
                    act.activation(v[:, :, 1, HD:2 * HD], src[:, :, 1, :], ACT.Copy).then_inc(v_ok, 1)
                b = st.b(-1)
                if b.within(B):
                    act.wait_ge(onT_ps, b.value(plus=1))
                    act.wait_ge(wo_ps, b.value())
                    act.activation(onT[:, :], ps_tok[:, 0:P], ACT.Copy).then_inc(onT_ok, 1)
                b = st.b(-2)
                if b.within(B):
                    act.wait_ge(q1_ps, b.value(plus=1))
                    act.wait_ge(prodk_ok, b.value())
                    act.activation(q1[:, :], ps_l1[:, 0:P], ACT.Copy).then_inc(q1_ok, 1)
                if s == 2 and g2.within(NG):
                    act.wait_ge(k_r, g2.value(plus=1))
                    act.activation(k3[:, 1, :], rk[:, :], ACT.Copy).then_inc(k_mid, 1)
                exps(3)
                b = st.b(-3)
                if b.within(B):
                    act.wait_ge(o1T_ps, b.value(plus=1))
                    act.wait_ge(wo1_ps, b.value())
                    act.activation(o1T[:, :], ps_l1[:, 0:P], ACT.Copy).then_inc(o1T_ok, 1)
                b = st.b(2)
                if b.within(B):
                    act.wait_ge(mT_ps, b.value(plus=1))
                    act.wait_ge(m_stacked, b.value(32))
                    act.activation(m_hi[:, :], ps_a[0][0:H, 0:P], ACT.Copy).then_inc(m_hi_ok, 1)
                b = st.b(1)
                if b.within(B):
                    gb = Count(b.first // GROUP, UNROLL // GROUP, b.it)
                    act.wait_ge(crs_ok, gb.value(plus=1))
                    act.wait_ge(selv_ps, b.value(plus=-3))
                    act.activation(kv1[b.first % 4][:, :], ps_prep[:, P:3 * P], ACT.Copy,
                                   scale=crs[gb.first % 2][:, b.first % GROUP:b.first % GROUP + 1]).then_inc(kv1_ok, 1)
                if cur.within(B):
                    act.wait_ge(pv_ps, cur.value(plus=1))
                    act.wait_ge(tok_ps, cur.value())
                    act.activation(pvs[:, :, :].rearrange("p a n -> p (a n)"), ps_tok[:, 0:2 * P], ACT.Copy).then_inc(pvs_ok, 1)
                if s == 0 and g2.within(NG):
                    act.wait_ge(q_ps, g2.value(plus=1))
                    act.wait_ge(q_written, g2.value(48))
                    act.activation(q3[:, 0, :], ps_prep[:, :], ACT.Identity, bias=cols[:, 0:1]).then_inc(q_hi, 1)

            run(act, step)

        @block.vector
        def _(dve):
            nc.vector.memset(qst[0][0:2 * E_ROWS, :, :, :].rearrange("p t e n -> p (t e n)").bitcast(F32), 0.0).then_inc(qst_zero, 1)
            dve.wait_ge(vec_in, 16 * 2)
            nc.vector.tensor_copy(bv_rep[:, :], cols[:, 2:3].to_broadcast([P, P])).then_inc(bv_ok, 1)

            def step(st):
                s = st.s
                ahead = st.b(2)
                g2 = st.g(2)
                if st.it is None and st.base == -1:
                    dve.wait_ge(c0_ps, 1)
                    nc.vector.tensor_tensor(c0[:, :], ps_tok[:, 0:P], rows_bc[:, 0, :], ALU.add).then_inc(c0_ok, 1)

                def maxima(c):
                    if ahead.within(B):
                        dve.wait_ge(a_ps, ahead.value(4, c + 1))
                        if c == 0:
                            dve.wait_ge(mT_ps, ahead.value())
                        nc.vector.tensor_reduce(negmax[:, 4 * c:4 * c + 4], ps_a[c % 2][:, :].rearrange("p (h k) -> p h k", h=4),
                                                AX.X, ALU.max, negate=True).then_inc(a_max, 1)

                maxima(0)
                a = st.b(-1)
                if a.within(B):
                    pair = ps_tok[:, 0:2 * P].rearrange("p (t c) -> p t c", c=32)
                    dve.wait_ge(tok_ps, a.value(plus=1))
                    nc.vector.reciprocal(rden[:, :, :], pair[:, :, 16:32:HD]).then_inc(rden_ok, 1)
                    dve.wait_ge(rden_ok, a.value(plus=1))
                    dve.wait_ge(onT_ps, a.value())
                    nc.vector.tensor_tensor(on[:, :].rearrange("p (t e d) -> p t e d", e=2, d=HD),
                                            pair[:, :, 0:16].rearrange("p t (e d) -> p t e d", d=HD),
                                            rden[:, :, :, None].to_broadcast([P, T, 2, HD]), ALU.mult).then_inc(on_ok, 1)
                maxima(1)
                maxima(2)
                if s == 1 and g2.within(NG):
                    dve.wait_ge(mask_in[g2.first % 2], g2.half().value(16, 16))
                    nc.vector.tensor_scalar(keep[:, :], maskb[g2.first % 2][:, :], 0.0, None, ALU.not_equal).then_inc(keep_ok, 1)
                if s == 2 and g2.within(NG):
                    g1 = st.g(1)
                    if g1.first >= 0:
                        dve.wait_ge(k_stacked[g1.first % 2], g1.half().value(48, 48))
                    nc.vector.tensor_scalar(mrow[0:1, :], maskb[g2.first % 2][0:1, :], 0.0, MASKED / SCALE, ALU.is_equal, ALU.mult).then_inc(mrow_ok, 1)
                g = st.g(1)
                if s == 3 and g.within(NG):
                    if g.first == 0:
                        dve.wait_ge(pool_setup, SETUP_OPS)
                    dve.wait_ge(idx_in[g.first % 2], g.half().value(16, 16))
                    dve.wait_ge(selv_ps, g.value(GROUP, -GROUP))
                    nc.vector.tensor_scalar(onehot[g.first % 2][:, 2, :], idxb[g.first % 2][:, :], pos[:, 2:3], None, ALU.is_equal).then_inc(onehot2_ok, 1)
                maxima(3)
                if a.within(B):
                    dve.wait_ge(wo_ps, a.value(plus=1))
                    dve.wait_ge(xb_ok, a.value(plus=1))
                    nc.vector.tensor_tensor(y[:, :], ps_tok[:, 0:P], xb[a.first % 2][:, :], ALU.add).then_inc(y_ok, 1)
                    dve.wait_ge(y_ok, a.value(plus=1))
                    nc.vector.bn_stats(bn[:, :], y[:, :]).then_inc(bn_ok, 1)
                    dve.wait_ge(bn_ok, a.value(plus=1))
                    dve.wait_ge(ve_ok, a.value())
                b = st.b(-2)
                if b.within(B):
                    dve.wait_ge(selk_ps, b.value(plus=1))
                    dve.wait_ge(q1_ok, b.value(plus=1))
                    nc.vector.tensor_tensor(prodk[:, :, :].rearrange("p (j h) d -> p j (h d)", j=3),
                                            ps_sel[:, 0:3 * P].rearrange("p (j n) -> p j n", j=3),
                                            q1[:, None, :].to_broadcast([P, 3, P]), ALU.mult).then_inc(prodk_ok, 1)
                if a.within(B):
                    nc.vector.bn_aggr(mv[:, :], bn[:, :]).then_inc(mv_ok, 1)
                if b.within(B):
                    dve.wait_ge(prodk_ok, b.value(plus=1))
                    nc.vector.tensor_reduce(s48[:, :], prodk[:, :, :], AX.X, ALU.add).then_inc(s48_ok, 1)
                c = st.b(-3)
                if c.within(B):
                    gc = Count(c.first // GROUP, UNROLL // GROUP, c.it)
                    dve.wait_ge(wo1_ps, c.value(plus=1))
                    if c.first % GROUP == 0:
                        dve.wait_ge(out_stored[gc.first % 2], gc.half().value(16))
                    nc.vector.tensor_tensor(outg[gc.first % 2][:, c.first % GROUP, :], ps_l1[:, 0:P],
                                            x1[c.first % 4][:, :], ALU.add).then_inc(out_ok, 1)
                def max_low():
                    if ahead.within(B):
                        dve.wait_ge(m_hi_ok, ahead.value(plus=1))
                        dve.wait_ge(m_stacked, ahead.value(32))
                        nc.vector.tensor_tensor(m_lo[:, :], ps_a[0][0:H, 0:P], m_hi[:, :], ALU.subtract).then_inc(m_lo_ok, 1)

                def standardize():
                    if a.within(B):
                        dve.wait_ge(rstd_ok, a.value(plus=1))
                        dve.wait_ge(t2_ok, a.value())
                        nc.vector.tensor_scalar(t1[:, :], y[:, :], mv[:, 0:1], rstd[:, :], ALU.subtract, ALU.mult).then_inc(t1_ok, 1)

                if b.within(B):
                    dve.wait_ge(s48_ok, b.value(plus=1))
                    nc.vector.scalar_tensor_tensor(out=w48[:, :, :].rearrange("p j h -> p (j h)"), in0=s48[:, :], scalar=0.0,
                                                   in1=s48[:, :], op0=ALU.max, op1=ALU.mult).then_inc(w48_ok, 1)
                    dve.wait_ge(w48_ok, b.value(plus=1))
                    nc.vector.tensor_reduce(den[:, :], w48[:, :, :].rearrange("p j h -> p h j"), AX.X, ALU.add).then_inc(den_ok, 1)
                max_low()
                if b.within(B):
                    dve.wait_ge(den_ok, b.value(plus=1))
                    dve.wait_ge(floor_ok, b.value(plus=1))
                    nc.vector.tensor_scalar(denm[:, :], den[:, :], floor[:, :], None, ALU.max).then_inc(denm_ok, 1)
                    dve.wait_ge(denm_ok, b.value(plus=1))
                    nc.vector.reciprocal(rec[:, :], denm[:, :]).then_inc(rec_ok, 1)
                standardize()
                if b.within(B):
                    dve.wait_ge(rec_ok, b.value(plus=1))
                    nc.vector.tensor_tensor(wn[:, :, :], w48[:, :, :], rec[:, None, :].to_broadcast([P, 3, H]), ALU.mult).then_inc(wn_ok, 1)
                if b.within(B):
                    dve.wait_ge(wn_ok, b.value(plus=1))
                    dve.wait_ge(selv_ps, b.value(plus=1))
                    dve.wait_ge(o1_ok, b.value())
                    nc.vector.tensor_tensor(prodv[:, :, :].rearrange("p j (h d) -> p (j h) d", d=HD),
                                            ps_sel[:, 0:3 * P].rearrange("p (c d) -> p c d", d=HD),
                                            wn[:, :, :].rearrange("p j h -> p (j h)")[:, :, None].to_broadcast([P, 3 * H, HD]),
                                            ALU.mult).then_inc(prodv_ok, 1)
                if s == 0 and g2.within(NG):
                    dve.wait_ge(q_hi, g2.value(plus=1))
                    dve.wait_ge(q_lo, g2.value())
                    nc.vector.scalar_tensor_tensor(out=rq[:, :], in0=ps_prep[:, :], scalar=cols[:, 0:1],
                                                   in1=q3[:, 0, :], op0=ALU.add, op1=ALU.subtract).then_inc(q_r, 1)
                if s == 1 and g2.within(NG):
                    dve.wait_ge(k_ps, g2.value(plus=1))
                    dve.wait_ge(keep_ok, g2.value(plus=1))
                    dve.wait_ge(k_r, g2.value())
                    nc.vector.scalar_tensor_tensor(out=kf[:, :], in0=ps_prep[:, :], scalar=cols[:, 1:2],
                                                   in1=keep[:, :], op0=ALU.add, op1=ALU.mult).then_inc(k_f, 1)

            run(dve, step)


_WEIGHTS = ('L0_xattn_Wv', 'L1_xattn_Wk', 'L1_xattn_Wv', 'L0_xattn_Wo', 'L1_xattn_Wq', 'L1_xattn_Wo')
_COLS = ('L0_xattn_bv', 'L1_xattn_gamma_q', 'L1_xattn_gamma_kv')
_ROWS = ('L0_xattn_bo', 'L0_xattn_ln_gamma', 'L0_xattn_ln_beta')


def kernel(**inputs):
    import numpy as _np
    import concourse.bacc as _bacc
    from concourse import mybir as _mybir
    from concourse.bass_utils import run_bass_kernel_spmd as _run

    a = {name: _np.asarray(v) for name, v in inputs.items()}
    x, ctx = a['x'], a['ctx_1024']
    shape, D = x.shape, x.shape[-1]

    def heads(w):
        return w.reshape(8, 2, D // 16, -1).transpose(1, 2, 0, 3).reshape(D, -1)

    laid_out = {
        "x": x,
        "xT": x.reshape(-1, D).T,
        "ctx": ctx,
        "ctxT": ctx.reshape(-1, D).T,
        "idx": a['itok_BxS_0_255'],
        "mask": a['mask_BxS2_if1'],
        "w_qk": _np.stack([heads(a['L0_xattn_Wq']).T, heads(a['L0_xattn_Wk']).T], axis=1),
        "w_rest": _np.stack([a[n].T for n in _WEIGHTS], axis=1),
        "cols": _np.concatenate([heads(a['L0_xattn_bq']), heads(a['L0_xattn_bk'])] + [a[n][:, None] for n in _COLS], axis=1),
        "rows": _np.stack([a[n] for n in _ROWS]),
    }

    nc = _bacc.Bacc("TRN2", target_bir_lowering=False, num_devices=1)
    arrays, args = {}, []
    for name, v in laid_out.items():
        v = _np.ascontiguousarray(v)
        arrays[f"in_{name}_dram"] = v
        args.append(nc.dram_tensor(f"in_{name}_dram", v.shape, _mybir.dt.from_np(v.dtype), kind="ExternalInput").ap())
    args.append(nc.dram_tensor("out_0_dram", shape, _mybir.dt.float32, kind="ExternalOutput").ap())
    xattn_kernel(nc, *args)
    r = _run(nc, [arrays], core_ids=[0])
    return r.results[0]["out_0_dram"]
```

```python
from contextlib import ExitStack

import concourse.bass as bass
from concourse import mybir

ALU = mybir.AluOpType
ACT = mybir.ActivationFunctionType
AX = mybir.AxisListType
F32 = mybir.dt.float32
BF16 = mybir.dt.bfloat16
I32 = mybir.dt.int32

LN_EPS = 1e-5
RMS_EPS = 1.1920929e-07
DEN_EPS = 1e-6
MASKED = -1e9

GROUP = 4
UNROLL = 2 * GROUP
TERMS = 6
RUNS = ((0, 3), (3, 2), (5, 1))


class Step:

    def __init__(self, base, it=None):
        self.base, self.it = base, it
        self.s = base % GROUP

    def b(self, lag):
        return Count(self.base + lag, UNROLL, self.it)

    def g(self, lag):
        return Count(self.base // GROUP + lag, UNROLL // GROUP, self.it)


class Count:

    def __init__(self, first, stride, it):
        self.first, self.stride, self.it = first, stride, it

    def within(self, n):
        return 0 <= self.first < n

    def value(self, times=1, plus=0):
        v = self.first * times + plus
        if self.it is None:
            return max(v, 0)
        assert v > 0
        return v + self.it * (self.stride * times)

    def half(self):
        return Count(self.first // 2, self.stride // 2, self.it)


def xattn_kernel(nc, x, xT_in, ctx, cT_in, idx, mask, w_qk, w_rest, cols_in, rows_in, out):
    B, S, D = x.shape
    H = 16
    HD = D // H
    T = H // 2
    NG = B // GROUP
    GT = GROUP * S
    E_ROWS = TERMS * HD
    MASK_ROW = 2 * E_ROWS
    M_ROW = MASK_ROW + 1
    A_ROWS = MASK_ROW + 1
    B_ROWS = M_ROW + 2
    CH = 4
    SCALE = float(HD) ** -0.5
    FLOOR_SCALE = DEN_EPS * HD
    SETUP_OPS = 14
    P = 128
    assert S == P and D == P and NG >= 8 and NG % 2 == 0

    es = ExitStack()
    with es:
        def sb(name, shape, dt=F32):
            return es.enter_context(nc.sbuf_tensor(name, shape, dt))

        def sem(name):
            return es.enter_context(nc.semaphore(name))

        def sems(name, n):
            return [sem(f"{name}{i}") for i in range(n)]

        q_scr = [nc.dram_tensor(f"q_scr{i}", [TERMS, D, GT], BF16).ap() for i in range(2)]
        k_scr = [nc.dram_tensor(f"k_scr{i}", [TERMS, D, GT], BF16).ap() for i in range(2)]

        ident = sb("ident", [P, P])
        wqk = sb("wqk", [P, 2, P])
        wrest = sb("wrest", [P, 6, P])
        woT, wq1T, wo1T = wrest[:, 3, :], wrest[:, 4, :], wrest[:, 5, :]
        cols = sb("cols", [P, 5])
        rows_bc = sb("rows_bc", [P, 3, P])
        ones = sb("ones", [2, GT], BF16)
        bv_rep = sb("bv_rep", [P, P])
        c0 = sb("c0", [P, P])
        pos = sb("pos", [P, 3])
        m_half = sb("m_half", [P, GROUP])
        eps = sb("eps", [P, GROUP + 2])

        xT = [sb(f"xT{i}", [P, GT]) for i in range(2)]
        cTk = [sb(f"cTk{i}", [P, GT]) for i in range(2)]
        cTv = [sb(f"cTv{i}", [P, GT]) for i in range(2)]
        cg = [sb(f"cg{i}", [P, GROUP, P]) for i in range(2)]
        xres = [sb(f"xres{i}", [P, GROUP, P]) for i in range(2)]
        maskb = [sb(f"maskb{i}", [P, GT], I32) for i in range(2)]
        idxb = [sb(f"idxb{i}", [P, GT], I32) for i in range(2)]
        onehot = [sb(f"onehot{i}", [P, 3, GT], BF16) for i in range(2)]
        keep = sb("keep", [P, GT])
        mrow = sb("mrow", [1, GT], BF16)
        q3 = sb("q3", [P, 3, GT], BF16)
        k3 = sb("k3", [P, 3, GT], BF16)
        rq = sb("rq", [P, GT])
        kf = sb("kf", [P, GT])
        rk = sb("rk", [P, GT])
        qst = [sb(f"qst{i}", [P, T, 2, GT], BF16) for i in range(2)]
        kst = [sb(f"kst{i}", [P, T, GT], BF16) for i in range(2)]
        cssq = [sb(f"cssq{i}", [P, GROUP]) for i in range(2)]
        cms = sb("cms", [P, GROUP])
        crs = [sb(f"crs{i}", [P, GROUP]) for i in range(2)]
        outg = [sb(f"outg{i}", [P, GROUP, P]) for i in range(2)]

        vpad = [sb(f"vpad{i}", [P, H, 32]) for i in range(2)]
        kv1 = [sb(f"kv1_{i}", [P, 2 * P]) for i in range(2)]
        rkv = [sb(f"rkv{i}", [P, 2 * P]) for i in range(2)]
        kv3 = [sb(f"kv3_{i}", [P, 3, 2 * P], BF16) for i in range(4)]
        negmax = sb("negmax", [P, H])
        m_hi = sb("m_hi", [H, P], BF16)
        m_lo = sb("m_lo", [H, P], BF16)
        probs = [sb(f"probs{i}", [P, CH, 4 * P]) for i in range(2)]
        pvs = sb("pvs", [P, 2, P])
        rden = sb("rden", [P, T, 2])
        on = sb("on", [P, P])
        onT = sb("onT", [P, P])
        xb = [sb(f"xb{i}", [P, P]) for i in range(2)]
        y = sb("y", [P, P])
        bn = sb("bn", [P, 6])
        mv = sb("mv", [P, 2])
        ve = sb("ve", [P, 1])
        nmu = sb("nmu", [P, 1])
        rstd = sb("rstd", [P, 1])
        nmr = sb("nmr", [P, 1])
        zero = sb("zero", [P, 1])
        t1 = sb("t1", [P, P])
        t2 = sb("t2", [P, P])
        x1 = [sb(f"x1_{i}", [P, P]) for i in range(4)]
        sq_c = sb("sq_c", [P, P])
        sq_x = sb("sq_x", [P, P])
        xssq = sb("xssq", [P, 1])
        floor = sb("floor", [P, 1])
        x1T = sb("x1T", [P, P])
        q1 = sb("q1", [P, P])
        prodk = sb("prodk", [P, 3 * H, HD])
        s48 = sb("s48", [P, 3 * H])
        w48 = sb("w48", [P, 3, H])
        den = sb("den", [P, H])
        denm = sb("denm", [P, H])
        rec = sb("rec", [P, H])
        wn = sb("wn", [P, 3, H])
        prodv = sb("prodv", [P, 3, P])
        o1a = sb("o1a", [P, P])
        o1 = sb("o1", [P, P])
        o1T = sb("o1T", [P, P])

        def bank(name):
            return es.enter_context(nc.psum_tensor(name, [P, 512], F32))

        ps_a = [bank("ps_a0"), bank("ps_a1")]
        ps_b = [bank("ps_b0"), bank("ps_b1")]
        ps_tok = bank("ps_tok")
        ps_prep = bank("ps_prep")
        ps_l1 = bank("ps_l1")
        ps_sel = bank("ps_sel")

        wqk_in, wrest_in, vec_in, ones_in = sem("wqk_in"), sem("wrest_in"), sem("vec_in"), sems("ones_in", 2)
        rows_loaded = sem("rows_loaded")
        pool_setup, ones_ok, qst_zero, vpad_ok = sem("pool_setup"), sem("ones_ok"), sem("qst_zero"), sem("vpad_ok")
        wt_ok, bv_ok, c0_ps, c0_ok = sem("wt_ok"), sem("bv_ok"), sem("c0_ps"), sem("c0_ok")
        x_in, ck_in, cv_in, c_in, mask_in = [sems(n, 2) for n in ("x_in", "ck_in", "cv_in", "c_in", "mask_in")]
        idx_in, xres_in = sems("idx_in", 2), sems("xres_in", 2)
        q_ps, q_hi, q_r, q_mid, q_lo = [sem(n) for n in ("q_ps", "q_hi", "q_r", "q_mid", "q_lo")]
        k_ps, k_f, k_hi, k_r, k_mid, k_lo = [sem(n) for n in ("k_ps", "k_f", "k_hi", "k_r", "k_mid", "k_lo")]
        keep_ok, mrow_ok = sem("keep_ok"), sem("mrow_ok")
        q_written, k_written = sem("q_written"), sem("k_written")
        q_stacked, k_stacked = sems("q_stacked", 2), sems("k_stacked", 2)
        cssq_ok, cms_ok, crs_ok = sem("cssq_ok"), sem("cms_ok"), sem("crs_ok")
        onehot_ok, onehot2_ok = sem("onehot_ok"), sem("onehot2_ok")
        vkv_ps, v_ok, kv1_ok = sem("vkv_ps"), sem("v_ok"), sem("kv1_ok")
        kv_hi, kv_r, kv_mid, kv_lo = [sem(n) for n in ("kv_hi", "kv_r", "kv_mid", "kv_lo")]
        a_ps, a_max, mT_ps, m_hi_ok, m_lo_ok, m_stacked = [sem(n) for n in ("a_ps", "a_max", "mT_ps", "m_hi_ok", "m_lo_ok", "m_stacked")]
        b_ps, exp_ok, pv_ps, pvs_ok = sem("b_ps"), sem("exp_ok"), sem("pv_ps"), sem("pvs_ok")
        tok_ps, rden_ok, on_ok, onT_ps, onT_ok, wo_ps = [sem(n) for n in ("tok_ps", "rden_ok", "on_ok", "onT_ps", "onT_ok", "wo_ps")]
        xb_ok, y_ok, bn_ok, mv_ok, ve_ok, nmu_ok, rstd_ok, nmr_ok, t1_ok, t2_ok, x1_ok = [sem(n) for n in (
            "xb_ok", "y_ok", "bn_ok", "mv_ok", "ve_ok", "nmu_ok", "rstd_ok", "nmr_ok", "t1_ok", "t2_ok", "x1_ok")]
        xssq_ok, floor_ok, o1a_ok = sem("xssq_ok"), sem("floor_ok"), sem("o1a_ok")
        x1T_ps, x1T_ok, q1_ps, q1_ok = sem("x1T_ps"), sem("x1T_ok"), sem("q1_ps"), sem("q1_ok")
        selk_ps, prodk_ok, s48_ok, w48_ok, den_ok, denm_ok, rec_ok, wn_ok = [sem(n) for n in (
            "selk_ps", "prodk_ok", "s48_ok", "w48_ok", "den_ok", "denm_ok", "rec_ok", "wn_ok")]
        selv_ps, prodv_ok, o1_ok, o1T_ps, o1T_ok, wo1_ps, out_ok = [sem(n) for n in (
            "selv_ps", "prodv_ok", "o1_ok", "o1T_ps", "o1T_ok", "wo1_ps", "out_ok")]
        out_stored = sems("out_stored", 2)

        FIRST, LOOP, LAST = -2 * GROUP, UNROLL, B + GROUP
        LOOPS = (B - 2 * GROUP - LOOP) // UNROLL

        def run(eng, step):
            for n in range(FIRST, LOOP):
                step(Step(n))
            with eng.Fori(0, LOOPS) as it:
                for s in range(UNROLL):
                    step(Step(LOOP + s, it))
            for n in range(LOOP + LOOPS * UNROLL, LAST):
                step(Step(n))

        def rows_of(tensor, g):
            at = g.value(GROUP)
            part = tensor[at:at + GROUP] if g.it is None else tensor[bass.ds(at, GROUP)]
            return part.rearrange("b s d -> s b d")

        def columns_of(tensor, g):
            at = g.value(GT)
            return tensor[:, at:at + GT] if g.it is None else tensor[:, bass.ds(at, GT)]

        def bcast_of(tensor, g):
            at = g.value(GT)
            flat = tensor.rearrange("(a b) s -> a (b s)", a=1)
            part = flat[:, at:at + GT] if g.it is None else flat[:, bass.ds(at, GT)]
            return part.to_broadcast([P, GT])

        block = es.enter_context(nc.Block())

        @block.sync
        def _(sp):
            sp.dma_start(wqk[:, :, :], w_qk).then_inc(wqk_in, 16)

            def write_q(scr, i):
                t0, n = RUNS[i]
                sp.dma_start(scr[t0:t0 + n].rearrange("t r n -> r t n"),
                             q3[:, i:i + 1, :].to_broadcast([P, n, GT])).then_inc(q_written, 16)

            def write_k(scr, i):
                t0, n = RUNS[i]
                sp.dma_start(scr[t0:t0 + n].rearrange("t r n -> r t n"), k3[:, 0:n, :]).then_inc(k_written, 16)

            def read_q(p):
                for e in range(2):
                    sp.dma_start(qst[p][E_ROWS * e:E_ROWS * (e + 1), :, e, :],
                                 head_rows(q_scr[p], e)).then_inc(q_stacked[p], 16)

            def read_k(p):
                for e in range(2):
                    sp.dma_start(kst[p][E_ROWS * e:E_ROWS * (e + 1), :, :].rearrange("p t n -> p (t n)"),
                                 head_rows(k_scr[p], e)).then_inc(k_stacked[p], 16)

            def copy_mask_row(p):
                sp.dma_start(kst[p][MASK_ROW:MASK_ROW + 1, :, :],
                             mrow[0:1, None, :].to_broadcast([1, T, GT])).then_inc(k_stacked[p], 16)

            def fill_constant_rows(p):
                sp.dma_start(qst[p][MASK_ROW:MASK_ROW + 1, :, :, :].rearrange("p t e n -> p (t e) n"),
                             ones[0:1, None, :].to_broadcast([1, 2 * T, GT])).then_inc(ones_in[p], 16)
                sp.dma_start(kst[p][M_ROW:M_ROW + 2, :, :],
                             ones[0:2, None, :].to_broadcast([2, T, GT])).then_inc(ones_in[p], 16)

            def load_idx(g, p):
                sp.dma_start(idxb[p][:, :], bcast_of(idx, g)).then_inc(idx_in[p], 16)

            def load_cTv(g, p):
                sp.dma_start(cTv[p][:, :], columns_of(cT_in, g)).then_inc(cv_in[p], 16)

            def head_rows(scr, e):
                return scr[:, HD * T * e:HD * T * (e + 1), :].rearrange("t (d a) n -> t d (a n)", a=T)

            def load_group(g, p):
                sp.dma_start(xT[p][:, :], columns_of(xT_in, g)).then_inc(x_in[p], 16)
                sp.dma_start(cTk[p][:, :], columns_of(cT_in, g)).then_inc(ck_in[p], 16)
                sp.dma_start(maskb[p][:, :], bcast_of(mask, g)).then_inc(mask_in[p], 16)

            def load_context(g, p):
                sp.dma_start(cg[p][:, :, :], rows_of(ctx, g)).then_inc(c_in[p], 16)

            def step(st):
                s = st.s
                if st.it is None and st.base == FIRST:
                    first, second = Count(0, 0, None), Count(1, 0, None)
                    load_group(first, 0)
                    load_context(first, 0)
                    load_group(second, 1)
                    sp.wait_ge(ones_ok, 1)
                    fill_constant_rows(0)
                    sp.wait_ge(q_hi, 1)
                    write_q(q_scr[0], 0)
                    sp.wait_ge(q_mid, 1)
                    write_q(q_scr[0], 1)
                    sp.wait_ge(q_lo, 1)
                    write_q(q_scr[0], 2)
                    sp.wait_ge(k_hi, 1)
                    write_k(k_scr[0], 2)
                    sp.dma_start(wrest[:, :, :], w_rest).then_inc(wrest_in, 16)
                    sp.wait_ge(k_mid, 1)
                    write_k(k_scr[0], 1)
                    sp.wait_ge(k_lo, 1)
                    write_k(k_scr[0], 0)
                    sp.wait_ge(q_written, 48)
                    sp.wait_ge(qst_zero, 2)
                    read_q(0)
                    sp.wait_ge(k_written, 48)
                    read_k(0)
                    sp.wait_ge(mrow_ok, 1)
                    copy_mask_row(0)
                    load_cTv(first, 0)
                    sp.dma_start(rows_bc[:, :, :].rearrange("p a n -> p (a n)"),
                                 rows_in.rearrange("(b a) n -> b (a n)", b=1).to_broadcast([P, 3 * P])).then_inc(rows_loaded, 16)
                    load_idx(first, 0)
                    load_context(second, 1)
                    fill_constant_rows(1)
                g = st.g(2)
                if s == 0 and g.first >= 2 and g.within(NG):
                    load_group(g, g.first % 2)
                b, g = st.b(1), st.g(1)
                if b.within(B):
                    qs = qst[(b.first // GROUP) % 2]
                    at = (b.first % GROUP) * S
                    for i, (m, ok) in enumerate(((m_hi, m_hi_ok), (m_lo, m_lo_ok))):
                        if i == 1 and s == 0 and g.within(NG):
                            sp.wait_ge(q_written, g.value(48, 48))
                        sp.wait_ge(ok, b.value(plus=1))
                        sp.dma_start(qs[M_ROW + i:M_ROW + i + 1, :, :, at:at + S].rearrange("p t e n -> p (t e) n"),
                                     m[:, :]).then_inc(m_stacked, 16)
                p, started = g.first % 2, g.first == 0
                if s == 0 and g.within(NG) and not started:
                    sp.wait_ge(k_lo, g.value(plus=1))
                    for i in range(3):
                        write_k(k_scr[p], i)
                    sp.wait_ge(b_ps, g.value(4 * GROUP, -4 * GROUP))
                    read_q(p)
                if s == 1 and g.within(NG) and not started:
                    sp.wait_ge(k_written, g.value(48, 48))
                    read_k(p)
                    sp.wait_ge(mrow_ok, g.value(plus=1))
                    copy_mask_row(p)
                    if g.first >= 2 or g.it is not None:
                        sp.wait_ge(vkv_ps, g.value(GROUP, -GROUP))
                    load_cTv(g, p)
                g = st.g(2)
                if s == 0 and g.first >= 2 and g.within(NG):
                    load_context(g, g.first % 2)
                p = g.first % 2
                started = g.first == 0
                if s == 1 and g.within(NG) and not started:
                    sp.wait_ge(q_lo, g.value(plus=1))
                    for i in range(3):
                        write_q(q_scr[p], i)
                if s == 3 and g.within(NG) and not started:
                    if g.first >= 2:
                        sp.wait_ge(onehot2_ok, g.value(plus=-1))
                        sp.wait_ge(onehot_ok, g.value(plus=-1))
                    load_idx(g, p)
                g = st.g(1)
                if s == 2 and g.within(NG):
                    sp.wait_ge(xb_ok, g.value(GROUP, -GROUP))
                    sp.dma_start(xres[g.first % 2][:, :, :], rows_of(x, g)).then_inc(xres_in[g.first % 2], 16)
                g = st.g(-1)
                if s == 3 and g.within(NG):
                    sp.wait_ge(out_ok, g.value(GROUP, GROUP))
                    sp.dma_start(rows_of(out, g), outg[g.first % 2][:, :, :]).then_inc(out_stored[g.first % 2], 16)

            run(sp, step)
            for p in range(2):
                sp.wait_ge(out_stored[p], 16 * (NG // 2))

        @block.gpsimd
        def _(pool):
            setup = [0]

            def alone(ins):
                ins.then_inc(pool_setup, 1)
                setup[0] += 1
                pool.wait_ge(pool_setup, setup[0])

            pool.memset(ones[:, :], 1.0).then_inc(ones_ok, 1)
            pool.memset(qst[1][0:2 * E_ROWS, :, :, :].rearrange("p t e n -> p (t e n)").bitcast(F32), 0.0).then_inc(qst_zero, 1)
            alone(pool.memset(ident[:, :], 0.0))
            alone(pool.affine_select(out=ident[:, :], in_=ident[:, :], compare_op=ALU.not_equal, fill=1.0,
                                     base=0, pattern=[[-1, P]], channel_multiplier=1))
            alone(pool.iota(pos[:, :], pattern=[[-1, 3]], base=1, channel_multiplier=1,
                            allow_small_or_imprecise_dtypes=True))
            alone(pool.memset(eps[:, 0:GROUP], RMS_EPS))
            alone(pool.memset(eps[:, GROUP:GROUP + 1], FLOOR_SCALE * RMS_EPS))
            alone(pool.memset(eps[:, GROUP + 1:GROUP + 2], LN_EPS))
            alone(pool.memset(m_half[:, :], -0.5))
            alone(pool.memset(zero[:, :], 0.0))
            for i in range(2):
                alone(pool.memset(vpad[i][:, :, :], 0.0))
                for e in range(2):
                    v = vpad[i][:, :, :].rearrange("p (t e) c -> p t e c", e=2)
                    alone(pool.memset(v[:, :, e, 16 + HD * e:16 + HD * (e + 1)], 1.0))
            pool.sem_inc(vpad_ok, 1)

            def power(dst, base, n, ok):
                return pool.tensor_tensor(dst, base, m_half[:, 0:n], ALU.pow).then_inc(ok, 1)

            def step(st):
                s = st.s
                hot_g = st.g(1) if s == 3 else st.g(0)
                hot = s in (3, 0) and hot_g.within(NG)
                b = st.b(-2)
                if b.within(B):
                    pool.wait_ge(t1_ok, b.value(plus=1))
                    pool.tensor_tensor(t2[:, :], t1[:, :], rows_bc[:, 1, :], ALU.mult).then_inc(t2_ok, 1)
                    if s == 3 and hot:
                        pool.wait_ge(idx_in[hot_g.first % 2], hot_g.half().value(16, 16))
                        pool.wait_ge(selv_ps, hot_g.value(GROUP, -GROUP))
                    pool.wait_ge(t2_ok, b.value(plus=1))
                    pool.wait_ge(out_ok, b.value(plus=-3))
                    pool.tensor_tensor(x1[b.first % 4][:, :], t2[:, :], rows_bc[:, 2, :], ALU.add).then_inc(x1_ok, 1)
                if s == 3 and hot and not st.b(-2).within(B):
                    pool.wait_ge(idx_in[hot_g.first % 2], hot_g.half().value(16, 16))
                if hot:
                    p, j = hot_g.first % 2, (0 if s == 3 else 1)
                    hot_j = pool.tensor_scalar(onehot[p][:, j, :], idxb[p][:, :], pos[:, j:j + 1], None, ALU.is_equal)
                    if j == 1:
                        hot_j.then_inc(onehot_ok, 1)
                b = st.b(-1)
                if b.within(B):
                    pool.wait_ge(kv_mid, b.value(plus=1))
                    pool.tensor_tensor(kv3[b.first % 4][:, 2, :], rkv[b.first % 2][:, :], kv3[b.first % 4][:, 1, :], ALU.subtract).then_inc(kv_lo, 1)
                g = st.g(1)
                p = g.first % 2
                if s == 1 and g.within(NG):
                    pool.wait_ge(cssq_ok, g.value(GROUP, GROUP))
                    pool.tensor_tensor(cms[:, :], cssq[p][:, :], eps[:, 0:GROUP], ALU.add).then_inc(cms_ok, 1)
                    pool.wait_ge(cms_ok, g.value(plus=1))
                    pool.wait_ge(kv1_ok, g.value(GROUP, -GROUP))
                    power(crs[p][:, :], cms[:, :], GROUP, crs_ok)
                b = st.b(-3)
                if b.within(B):
                    pool.wait_ge(prodv_ok, b.value(plus=1))
                    pool.tensor_tensor(o1a[:, :], prodv[:, 0, :], prodv[:, 1, :], ALU.add).then_inc(o1a_ok, 1)
                    pool.wait_ge(o1a_ok, b.value(plus=1))
                    pool.wait_ge(o1T_ps, b.value())
                    pool.tensor_tensor(o1[:, :], o1a[:, :], prodv[:, 2, :], ALU.add).then_inc(o1_ok, 1)
                b = st.b(0)
                if b.within(B):
                    g = st.g(0)
                    if s == 0:
                        pool.wait_ge(xres_in[g.first % 2], g.half().value(16, 16))
                    if b.first == 0:
                        pool.wait_ge(c0_ok, 1)
                    pool.wait_ge(y_ok, b.value(plus=-1))
                    pool.tensor_tensor(xb[b.first % 2][:, :], xres[g.first % 2][:, s, :], c0[:, :], ALU.add).then_inc(xb_ok, 1)
                b = st.b(0)
                if b.within(B):
                    pool.wait_ge(kv_hi, b.value(plus=1))
                    pool.wait_ge(kv_mid, b.value(plus=-1))
                    pool.tensor_tensor(rkv[b.first % 2][:, :], kv1[b.first % 2][:, :], kv3[b.first % 4][:, 0, :], ALU.subtract).then_inc(kv_r, 1)
                b = st.b(-2)
                if b.within(B):
                    pool.wait_ge(xssq_ok, b.value(plus=1))
                    pool.wait_ge(denm_ok, b.value())
                    pool.tensor_tensor(floor[:, :], xssq[:, :], eps[:, GROUP:GROUP + 1], ALU.add).then_inc(floor_ok, 1)
                b = st.b(-1)
                if b.within(B):
                    pool.wait_ge(mv_ok, b.value(plus=1))
                    pool.tensor_tensor(ve[:, :], mv[:, 1:2], eps[:, GROUP + 1:GROUP + 2], ALU.add).then_inc(ve_ok, 1)
                    pool.wait_ge(nmr_ok, b.value())
                    pool.tensor_tensor(nmu[:, :], zero[:, :], mv[:, 0:1], ALU.subtract).then_inc(nmu_ok, 1)
                    pool.wait_ge(ve_ok, b.value(plus=1))
                    pool.wait_ge(t1_ok, b.value())
                    power(rstd[:, :], ve[:, :], 1, rstd_ok)
                    pool.wait_ge(nmu_ok, b.value(plus=1))
                    pool.wait_ge(rstd_ok, b.value(plus=1))
                    pool.tensor_tensor(nmr[:, :], nmu[:, :], rstd[:, :], ALU.mult).then_inc(nmr_ok, 1)
                g = st.g(2)
                if s == 2 and g.within(NG):
                    pool.wait_ge(k_hi, g.value(plus=1))
                    pool.wait_ge(k_mid, g.value())
                    pool.tensor_tensor(rk[:, :], kf[:, :], k3[:, 0, :], ALU.subtract).then_inc(k_r, 1)
                if s == 3 and g.within(NG):
                    pool.wait_ge(k_mid, g.value(plus=1))
                    pool.tensor_tensor(k3[:, 2, :], rk[:, :], k3[:, 1, :], ALU.subtract).then_inc(k_lo, 1)
                if s == 1 and g.within(NG):
                    pool.wait_ge(q_mid, g.value(plus=1))
                    pool.tensor_tensor(q3[:, 2, :], rq[:, :], q3[:, 1, :], ALU.subtract).then_inc(q_lo, 1)

            run(pool, step)

        @block.tensor
        def _(pe):
            pe.wait_ge(wqk_in, 16)

            def step(st):
                s = st.s
                cur, ahead, after = st.b(0), st.b(2), st.b(-1)

                def scores_kq(c):
                    if not cur.within(B):
                        return
                    p, at = (cur.first // GROUP) % 2, s * S
                    if c == 0:
                        pe.wait_ge(m_stacked, cur.value(32, 32))
                    pe.wait_ge(exp_ok, cur.value(4, c - 1))
                    for i in range(2):
                        t = 2 * c + i
                        last = nc.tensor.matmul(ps_b[c % 2][:, 2 * P * i:2 * P * (i + 1)],
                                                kst[p][0:B_ROWS, t, at:at + S],
                                                qst[p][0:B_ROWS, t, :, at:at + S], start=True, stop=True)
                    last.then_inc(b_ps, 1)

                def scores_qk(c):
                    if not ahead.within(B):
                        return
                    p, at = (ahead.first // GROUP) % 2, (ahead.first % GROUP) * S
                    if c == 0 and ahead.it is None and ahead.first in (0, GROUP):
                        pe.wait_ge(ones_in[p], 16 * 2)
                    if c == 0 and ahead.it is None and ahead.first == 0:
                        pe.wait_ge(pool_setup, SETUP_OPS)
                    if c == 0 and at == 0:
                        gh = st.g(1).half()
                        pe.wait_ge(q_stacked[p], gh.value(32, 32))
                        pe.wait_ge(k_stacked[p], gh.value(48, 48))
                    if c == 0:
                        pe.wait_ge(m_hi_ok, ahead.value())
                        pe.wait_ge(m_lo_ok, ahead.value())
                    else:
                        pe.wait_ge(a_max, ahead.value(4, 0 if c == 1 else c - 1))
                    for h in range(4 * c, 4 * c + 4):
                        t, e = h // 2, h % 2
                        last = nc.tensor.matmul(ps_a[c % 2][:, (h % 4) * P:(h % 4 + 1) * P],
                                                qst[p][0:A_ROWS, t, e, at:at + S],
                                                kst[p][0:A_ROWS, t, at:at + S], start=True, stop=True)
                    last.then_inc(a_ps, 1)

                def max_rows():
                    if ahead.within(B):
                        pe.wait_ge(a_max, ahead.value(4, 4))
                        nc.tensor.matmul(ps_a[0][0:H, 0:P], negmax[:, :], ident[:, :], start=True, stop=True).then_inc(mT_ps, 1)

                def values():
                    if not cur.within(B):
                        return
                    pe.wait_ge(v_ok, cur.value(plus=1))
                    if cur.it is None and cur.first == 0:
                        pe.wait_ge(c0_ok, 1)
                    pe.wait_ge(y_ok, cur.value())
                    for half in range(2):
                        pe.wait_ge(exp_ok, cur.value(4, 2 * half + 2))
                        for e in range(2):
                            for j in range(4):
                                h = 8 * half + 2 * j + e
                                last = nc.tensor.matmul(ps_tok[32 * j:32 * j + 32, P * half:P * (half + 1)],
                                                        vpad[cur.first % 2][:, h, :],
                                                        probs[cur.first % 2][:, h // 4, (h % 4) * P:(h % 4 + 1) * P],
                                                        start=(e == 0), stop=(e == 1))
                    last.then_inc(pv_ps, 1)

                def to_tokens():
                    if after.within(B):
                        pe.wait_ge(pvs_ok, after.value(plus=1))
                        for half in range(2):
                            last = nc.tensor.transpose(ps_tok[:, P * half:P * (half + 1)], pvs[:, half, :], ident[:, :])
                        last.then_inc(tok_ps, 1)

                def to_features():
                    if after.within(B):
                        pe.wait_ge(on_ok, after.value(plus=1))
                        nc.tensor.transpose(ps_tok[:, 0:P], on[:, :], ident[:, :]).then_inc(onT_ps, 1)

                def out_proj0():
                    if after.within(B):
                        pe.wait_ge(onT_ok, after.value(plus=1))
                        nc.tensor.matmul(ps_tok[:, 0:P], onT[:, :], woT, start=True, stop=True).then_inc(wo_ps, 1)

                def l1_transpose():
                    b = st.b(-2)
                    if b.within(B):
                        pe.wait_ge(x1_ok, b.value(plus=1))
                        pe.wait_ge(out_ok, b.value(plus=-1))
                        nc.tensor.transpose(ps_l1[:, 0:P], x1[b.first % 4][:, :], ident[:, :]).then_inc(x1T_ps, 1)

                def l1_query():
                    b = st.b(-2)
                    if b.within(B):
                        pe.wait_ge(x1T_ok, b.value(plus=1))
                        nc.tensor.matmul(ps_l1[:, 0:P], x1T[:, :], wq1T, start=True, stop=True).then_inc(q1_ps, 1)

                def select(which, done):
                    b = st.b(-2 - which)
                    if not b.within(B):
                        return
                    i = b.first % GROUP
                    if which == 0:
                        if i == 0:
                            pe.wait_ge(onehot_ok, st.g(0).value(plus=1))
                            pe.wait_ge(onehot2_ok, st.g(0).value(plus=1))
                        pe.wait_ge(prodv_ok, b.value())
                        pe.wait_ge(kv_lo, b.value(plus=1))
                    else:
                        pe.wait_ge(prodk_ok, b.value(plus=1))
                    for j in range(3):
                        for part in range(3):
                            last = nc.tensor.matmul(ps_sel[:, P * j:P * (j + 1)],
                                                    onehot[(b.first // GROUP) % 2][:, j, i * S:(i + 1) * S],
                                                    kv3[b.first % 4][:, part, P * which:P * (which + 1)],
                                                    start=(part == 0), stop=(part == 2))
                    last.then_inc(done, 1)

                def l1_out_transpose():
                    b = st.b(-3)
                    if b.within(B):
                        pe.wait_ge(o1_ok, b.value(plus=1))
                        if st.b(-2).within(B):
                            pe.wait_ge(q1_ok, st.b(-2).value(plus=1))
                        else:
                            pe.wait_ge(out_ok, b.value())
                        nc.tensor.transpose(ps_l1[:, 0:P], o1[:, :], ident[:, :]).then_inc(o1T_ps, 1)

                def l1_out_proj():
                    b = st.b(-3)
                    if b.within(B):
                        pe.wait_ge(o1T_ok, b.value(plus=1))
                        nc.tensor.matmul(ps_l1[:, 0:P], o1T[:, :], wo1T, start=True, stop=True).then_inc(wo1_ps, 1)

                def project_ctx():
                    b = st.b(1)
                    if not b.within(B):
                        return
                    i, p = b.first % GROUP, (b.first // GROUP) % 2
                    gb = Step(st.base - 1, st.it).g(2)
                    if s == 1 and gb.within(NG):
                        pe.wait_ge(q_r, gb.value(plus=1))
                    elif s == 2 and gb.within(NG):
                        pe.wait_ge(k_f, gb.value(plus=1))
                    else:
                        pe.wait_ge(kv1_ok, b.value())
                    if i == 0:
                        gh = Count(b.first // GROUP, UNROLL // GROUP, b.it).half()
                        pe.wait_ge(cv_in[p], gh.value(16, 16))
                    nc.tensor.matmul(ps_prep[:, 0:3 * P], cTv[p][:, i * S:(i + 1) * S],
                                     wrest[:, 0:3, :], start=True, stop=True).then_inc(vkv_ps, 1)

                def group_piece():
                    g = st.g(2)
                    if s > 1 or not g.within(NG):
                        return
                    p = g.first % 2
                    if st.b(1).within(B):
                        pe.wait_ge(kv1_ok, st.b(1).value(plus=1))
                    early = st.it is None and st.base < 0
                    k_bank = ps_l1 if early else ps_prep
                    if s == 0:
                        pe.wait_ge(x_in[p], g.half().value(16, 16))
                        pe.wait_ge(q_r, g.value())
                        nc.tensor.matmul(ps_prep[:, :], wqk[:, 0, :], xT[p][:, :], start=True, stop=True).then_inc(q_ps, 1)
                    else:
                        pe.wait_ge(ck_in[p], g.half().value(16, 16))
                        pe.wait_ge(k_f, g.value())
                        nc.tensor.matmul(k_bank[:, :], wqk[:, 1, :], cTk[p][:, :], start=True, stop=True).then_inc(k_ps, 1)

                if st.it is None and st.base == -2:
                    pe.wait_ge(bv_ok, 1)
                    pe.wait_ge(wt_ok, 1)
                    nc.tensor.matmul(ps_tok[:, 0:P], bv_rep[:, :], woT, start=True, stop=True).then_inc(c0_ps, 1)
                early = st.it is None and st.base < 0
                if early:
                    project_ctx()
                to_tokens()
                scores_kq(0)
                scores_qk(0)
                scores_kq(1)
                scores_qk(1)
                to_features()
                select(1, selv_ps)
                l1_transpose()
                scores_kq(2)
                out_proj0()
                scores_qk(2)
                l1_query()
                scores_kq(3)
                select(0, selk_ps)
                scores_qk(3)
                if s < 2 and not early:
                    project_ctx()
                l1_out_transpose()
                values()
                l1_out_proj()
                max_rows()
                if s >= 2 and not early:
                    project_ctx()
                group_piece()

            run(pe, step)

        @block.scalar
        def _(act):
            with nc.allow_non_contiguous_dma("five numbers a partition, once"):
                act.dma_start(cols[:, :], cols_in).then_inc(vec_in, 16)
            act.wait_ge(vec_in, 16)
            act.activation(bv_rep[:, :], cols[:, 2:3].to_broadcast([P, P]), ACT.Copy).then_inc(bv_ok, 1)

            def scale_weights():
                act.wait_ge(wrest_in, 16)
                kv = wrest[:, 1:3, :].rearrange("p a n -> p (a n)")
                act.activation(kv, kv, ACT.Copy, scale=cols[:, 4:5])
                act.activation(wq1T, wq1T, ACT.Copy, scale=cols[:, 3:4]).then_inc(wt_ok, 1)

            def step(st):
                s = st.s
                cur = st.b(0)
                g2 = st.g(2)

                def exps(c):
                    if cur.within(B):
                        act.wait_ge(b_ps, cur.value(4, c + 1))
                        if c == 0:
                            act.wait_ge(pv_ps, cur.value(plus=-1))
                        act.activation(probs[cur.first % 2][:, c, :], ps_b[c % 2][:, :], ACT.Exp, scale=SCALE).then_inc(exp_ok, 1)

                def context_rows():
                    b = st.b(1)
                    if b.within(B):
                        if b.it is None and b.first == 0:
                            act.wait_ge(vpad_ok, 1)
                        act.wait_ge(vkv_ps, b.value(plus=1))
                        act.wait_ge(pv_ps, b.value(plus=-1))
                        v = vpad[b.first % 2][:, :, :].rearrange("p (t e) c -> p t e c", e=2)
                        src = ps_prep[:, 0:P].rearrange("p (t e d) -> p t e d", e=2, d=HD)
                        act.activation(v[:, :, 0, 0:HD], src[:, :, 0, :], ACT.Copy)
                        act.activation(v[:, :, 1, HD:2 * HD], src[:, :, 1, :], ACT.Copy).then_inc(v_ok, 1)
                    b = st.b(1)
                    if b.within(B):
                        gb = Count(b.first // GROUP, UNROLL // GROUP, b.it)
                        act.wait_ge(crs_ok, gb.value(plus=1))
                        act.wait_ge(kv_r, b.value(plus=-1))
                        act.activation(kv1[b.first % 2][:, :], ps_prep[:, P:3 * P], ACT.Copy,
                                       scale=crs[gb.first % 2][:, b.first % GROUP:b.first % GROUP + 1]).then_inc(kv1_ok, 1)

                if st.it is None and st.base == FIRST + 4:
                    scale_weights()
                exps(0)
                b = st.b(-1)
                if b.within(B):
                    act.wait_ge(onT_ps, b.value(plus=1))
                    act.wait_ge(wo_ps, b.value())
                    act.activation(onT[:, :], ps_tok[:, 0:P], ACT.Copy).then_inc(onT_ok, 1)
                exps(1)
                b = st.b(-2)
                if b.within(B):
                    act.wait_ge(x1T_ps, b.value(plus=1))
                    act.wait_ge(q1_ps, b.value())
                    act.activation(x1T[:, :], ps_l1[:, 0:P], ACT.Copy).then_inc(x1T_ok, 1)
                exps(2)
                if s == 3 and g2.within(NG):
                    act.wait_ge(k_r, g2.value(plus=1))
                    act.activation(k3[:, 1, :], rk[:, :], ACT.Copy).then_inc(k_mid, 1)
                b = st.b(-2)
                if b.within(B):
                    act.wait_ge(x1_ok, b.value(plus=1))
                    act.wait_ge(floor_ok, b.value())
                    act.wait_ge(xssq_ok, b.value())
                    act.activation(sq_x[:, :], x1[b.first % 4][:, :], ACT.Square, scale=(FLOOR_SCALE / D) ** 0.5, accum_out=xssq[:, :]).then_inc(xssq_ok, 1)
                b = st.b(-2)
                if b.within(B):
                    act.wait_ge(q1_ps, b.value(plus=1))
                    act.wait_ge(prodk_ok, b.value())
                    act.activation(q1[:, :], ps_l1[:, 0:P], ACT.Copy).then_inc(q1_ok, 1)
                if s == 1 and g2.within(NG):
                    act.wait_ge(q_r, g2.value(plus=1))
                    act.activation(q3[:, 1, :], rq[:, :], ACT.Copy).then_inc(q_mid, 1)
                exps(3)
                if s == 2 and g2.within(NG):
                    act.wait_ge(k_f, g2.value(plus=1))
                    act.wait_ge(k_written, g2.value(48))
                    act.activation(k3[:, 0, :], kf[:, :], ACT.Copy).then_inc(k_hi, 1)
                b = st.b(2 * GROUP - 1)
                if b.within(B):
                    gb = Count(b.first // GROUP, UNROLL // GROUP, b.it)
                    p, i = gb.first % 2, b.first % GROUP
                    if i == 0:
                        act.wait_ge(c_in[p], gb.half().value(16, 16))
                        act.wait_ge(cms_ok, gb.value(plus=-1))
                    act.wait_ge(cssq_ok, b.value())
                    act.activation(sq_c[:, :], cg[p][:, i, :], ACT.Square, scale=float(D) ** -0.5, accum_out=cssq[p][:, i:i + 1]).then_inc(cssq_ok, 1)
                early = st.it is None and st.base < 0
                if s < 2 or early:
                    context_rows()
                b = st.b(-3)
                if b.within(B):
                    act.wait_ge(o1T_ps, b.value(plus=1))
                    act.wait_ge(wo1_ps, b.value())
                    act.activation(o1T[:, :], ps_l1[:, 0:P], ACT.Copy).then_inc(o1T_ok, 1)
                if cur.within(B):
                    act.wait_ge(pv_ps, cur.value(plus=1))
                    act.wait_ge(tok_ps, cur.value())
                    act.activation(pvs[:, :, :].rearrange("p a n -> p (a n)"), ps_tok[:, 0:2 * P], ACT.Copy).then_inc(pvs_ok, 1)
                b = st.b(2)
                if b.within(B):
                    act.wait_ge(mT_ps, b.value(plus=1))
                    act.wait_ge(m_stacked, b.value(32))
                    act.activation(m_hi[:, :], ps_a[0][0:H, 0:P], ACT.Copy).then_inc(m_hi_ok, 1)
                b = st.b(-1)
                if b.within(B):
                    act.wait_ge(rstd_ok, b.value(plus=1))
                    act.wait_ge(nmr_ok, b.value(plus=1))
                    act.wait_ge(t2_ok, b.value())
                    act.activation(t1[:, :], y[:, :], ACT.Identity, bias=nmr[:, :], scale=rstd[:, :]).then_inc(t1_ok, 1)
                if s >= 2 and not early:
                    context_rows()
                if cur.within(B):
                    act.wait_ge(kv_r, cur.value(plus=1))
                    act.activation(kv3[cur.first % 4][:, 1, :], rkv[cur.first % 2][:, :], ACT.Copy).then_inc(kv_mid, 1)
                b = st.b(1)
                if b.within(B):
                    act.wait_ge(kv1_ok, b.value(plus=1))
                    act.wait_ge(selv_ps, b.value(plus=-3))
                    act.activation(kv3[b.first % 4][:, 0, :], kv1[b.first % 2][:, :], ACT.Copy).then_inc(kv_hi, 1)
                if s == 0 and g2.within(NG):
                    act.wait_ge(q_ps, g2.value(plus=1))
                    act.wait_ge(q_written, g2.value(48))
                    act.activation(q3[:, 0, :], ps_prep[:, :], ACT.Identity, bias=cols[:, 0:1]).then_inc(q_hi, 1)

            run(act, step)

        @block.vector
        def _(dve):
            nc.vector.memset(qst[0][0:2 * E_ROWS, :, :, :].rearrange("p t e n -> p (t e n)").bitcast(F32), 0.0).then_inc(qst_zero, 1)
            dve.wait_ge(vec_in, 16)

            def step(st):
                s = st.s
                ahead = st.b(2)
                g2 = st.g(2)
                if st.it is None and st.base == -1:
                    dve.wait_ge(c0_ps, 1)
                    dve.wait_ge(rows_loaded, 16)
                    nc.vector.tensor_tensor(c0[:, :], ps_tok[:, 0:P], rows_bc[:, 0, :], ALU.add).then_inc(c0_ok, 1)

                def maxima(c):
                    if ahead.within(B):
                        dve.wait_ge(a_ps, ahead.value(4, c + 1))
                        if c == 0:
                            dve.wait_ge(mT_ps, ahead.value())
                        nc.vector.tensor_reduce(negmax[:, 4 * c:4 * c + 4], ps_a[c % 2][:, :].rearrange("p (h k) -> p h k", h=4),
                                                AX.X, ALU.max, negate=True).then_inc(a_max, 1)

                def max_low():
                    if ahead.within(B):
                        dve.wait_ge(m_hi_ok, ahead.value(plus=1))
                        dve.wait_ge(m_stacked, ahead.value(32))
                        nc.vector.tensor_tensor(m_lo[:, :], ps_a[0][0:H, 0:P], m_hi[:, :], ALU.subtract).then_inc(m_lo_ok, 1)

                a, b, c = st.b(-1), st.b(-2), st.b(-3)
                pair = ps_tok[:, 0:2 * P].rearrange("p (t c) -> p t c", c=32)

                early = st.it is None and st.base < 0

                def masked_k():
                    if s == 2 and g2.within(NG):
                        dve.wait_ge(k_ps, g2.value(plus=1))
                        dve.wait_ge(keep_ok, g2.value(plus=1))
                        dve.wait_ge(k_r, g2.value())
                        k_bank = ps_l1 if early else ps_prep
                        nc.vector.scalar_tensor_tensor(out=kf[:, :], in0=k_bank[:, :], scalar=cols[:, 1:2],
                                                       in1=keep[:, :], op0=ALU.add, op1=ALU.mult).then_inc(k_f, 1)

                def mask_row_and_onehot():
                    if s == 3 and g2.within(NG):
                        g1 = st.g(1)
                        if g1.first >= 0:
                            dve.wait_ge(k_stacked[g1.first % 2], g1.half().value(48, 48))
                        nc.vector.tensor_scalar(mrow[0:1, :], maskb[g2.first % 2][0:1, :], 0.0, MASKED / SCALE, ALU.is_equal, ALU.mult).then_inc(mrow_ok, 1)
                    g = st.g(1)
                    if s == 3 and g.within(NG):
                        if g.first == 0:
                            dve.wait_ge(pool_setup, SETUP_OPS)
                        dve.wait_ge(idx_in[g.first % 2], g.half().value(16, 16))
                        dve.wait_ge(selv_ps, g.value(GROUP, -GROUP))
                        nc.vector.tensor_scalar(onehot[g.first % 2][:, 2, :], idxb[g.first % 2][:, :], pos[:, 2:3], None, ALU.is_equal).then_inc(onehot2_ok, 1)

                if early:
                    masked_k()
                    mask_row_and_onehot()

                if a.within(B):
                    dve.wait_ge(tok_ps, a.value(plus=1))
                    nc.vector.reciprocal(rden[:, :, :], pair[:, :, 16:32:HD]).then_inc(rden_ok, 1)
                if a.within(B):
                    dve.wait_ge(rden_ok, a.value(plus=1))
                    dve.wait_ge(onT_ps, a.value())
                    nc.vector.tensor_tensor(on[:, :].rearrange("p (t e d) -> p t e d", e=2, d=HD),
                                            pair[:, :, 0:16].rearrange("p t (e d) -> p t e d", d=HD),
                                            rden[:, :, :, None].to_broadcast([P, T, 2, HD]), ALU.mult).then_inc(on_ok, 1)
                if c.within(B):
                    dve.wait_ge(den_ok, c.value(plus=1))
                    dve.wait_ge(floor_ok, c.value(plus=1))
                    nc.vector.tensor_scalar(denm[:, :], den[:, :], floor[:, :], None, ALU.max).then_inc(denm_ok, 1)
                maxima(0)
                if c.within(B):
                    dve.wait_ge(denm_ok, c.value(plus=1))
                    nc.vector.reciprocal(rec[:, :], denm[:, :]).then_inc(rec_ok, 1)
                maxima(1)
                if c.within(B):
                    dve.wait_ge(rec_ok, c.value(plus=1))
                    nc.vector.tensor_tensor(wn[:, :, :], w48[:, :, :], rec[:, None, :].to_broadcast([P, 3, H]), ALU.mult).then_inc(wn_ok, 1)
                if c.within(B):
                    dve.wait_ge(wn_ok, c.value(plus=1))
                    dve.wait_ge(selv_ps, c.value(plus=1))
                    dve.wait_ge(o1_ok, c.value())
                    nc.vector.tensor_tensor(prodv[:, :, :].rearrange("p j (h d) -> p (j h) d", d=HD),
                                            ps_sel[:, 0:3 * P].rearrange("p (c d) -> p c d", d=HD),
                                            wn[:, :, :].rearrange("p j h -> p (j h)")[:, :, None].to_broadcast([P, 3 * H, HD]),
                                            ALU.mult).then_inc(prodv_ok, 1)
                if s == 1 and g2.within(NG):
                    dve.wait_ge(q_hi, g2.value(plus=1))
                    dve.wait_ge(q_lo, g2.value())
                    nc.vector.scalar_tensor_tensor(out=rq[:, :], in0=ps_prep[:, :], scalar=cols[:, 0:1],
                                                   in1=q3[:, 0, :], op0=ALU.add, op1=ALU.subtract).then_inc(q_r, 1)
                if not early:
                    masked_k()
                if a.within(B):
                    dve.wait_ge(wo_ps, a.value(plus=1))
                    dve.wait_ge(xb_ok, a.value(plus=1))
                    dve.wait_ge(t1_ok, a.value())
                    nc.vector.tensor_tensor(y[:, :], ps_tok[:, 0:P], xb[a.first % 2][:, :], ALU.add).then_inc(y_ok, 1)
                maxima(2)
                if a.within(B):
                    dve.wait_ge(y_ok, a.value(plus=1))
                    nc.vector.bn_stats(bn[:, :], y[:, :]).then_inc(bn_ok, 1)
                if s == 1 and g2.within(NG):
                    dve.wait_ge(mask_in[g2.first % 2], g2.half().value(16, 16))
                    nc.vector.tensor_scalar(keep[:, :], maskb[g2.first % 2][:, :], 0.0, None, ALU.not_equal).then_inc(keep_ok, 1)
                if not early:
                    mask_row_and_onehot()
                if a.within(B):
                    dve.wait_ge(bn_ok, a.value(plus=1))
                    dve.wait_ge(nmu_ok, a.value())
                if b.within(B):
                    dve.wait_ge(selk_ps, b.value(plus=1))
                    dve.wait_ge(q1_ok, b.value(plus=1))
                    nc.vector.tensor_tensor(prodk[:, :, :].rearrange("p (j h) d -> p j (h d)", j=3),
                                            ps_sel[:, 0:3 * P].rearrange("p (j n) -> p j n", j=3),
                                            q1[:, None, :].to_broadcast([P, 3, P]), ALU.mult).then_inc(prodk_ok, 1)
                if a.within(B):
                    nc.vector.bn_aggr(mv[:, :], bn[:, :]).then_inc(mv_ok, 1)
                maxima(3)
                if b.within(B):
                    dve.wait_ge(prodk_ok, b.value(plus=1))
                    nc.vector.tensor_reduce(s48[:, :], prodk[:, :, :], AX.X, ALU.add).then_inc(s48_ok, 1)
                    dve.wait_ge(s48_ok, b.value(plus=1))
                    nc.vector.scalar_tensor_tensor(out=w48[:, :, :].rearrange("p j h -> p (j h)"), in0=s48[:, :], scalar=0.0,
                                                   in1=s48[:, :], op0=ALU.max, op1=ALU.mult).then_inc(w48_ok, 1)
                if b.within(B):
                    dve.wait_ge(w48_ok, b.value(plus=1))
                    nc.vector.tensor_reduce(den[:, :], w48[:, :, :].rearrange("p j h -> p h j"), AX.X, ALU.add).then_inc(den_ok, 1)
                if c.within(B):
                    gc = Count(c.first // GROUP, UNROLL // GROUP, c.it)
                    dve.wait_ge(wo1_ps, c.value(plus=1))
                    if c.first % GROUP == 0:
                        dve.wait_ge(out_stored[gc.first % 2], gc.half().value(16))
                    nc.vector.tensor_tensor(outg[gc.first % 2][:, c.first % GROUP, :], ps_l1[:, 0:P],
                                            x1[c.first % 4][:, :], ALU.add).then_inc(out_ok, 1)
                max_low()

            run(dve, step)


_WEIGHTS = ('L0_xattn_Wv', 'L1_xattn_Wk', 'L1_xattn_Wv', 'L0_xattn_Wo', 'L1_xattn_Wq', 'L1_xattn_Wo')
_COLS = ('L0_xattn_bv', 'L1_xattn_gamma_q', 'L1_xattn_gamma_kv')
_ROWS = ('L0_xattn_bo', 'L0_xattn_ln_gamma', 'L0_xattn_ln_beta')


def kernel(**inputs):
    import numpy as _np
    import concourse.bacc as _bacc
    from concourse import mybir as _mybir
    from concourse.bass_utils import run_bass_kernel_spmd as _run

    a = {name: _np.asarray(v) for name, v in inputs.items()}
    x, ctx = a['x'], a['ctx_1024']
    shape, D = x.shape, x.shape[-1]

    def heads(w):
        return w.reshape(8, 2, D // 16, -1).transpose(1, 2, 0, 3).reshape(D, -1)

    laid_out = {
        "x": x,
        "xT": x.reshape(-1, D).T,
        "ctx": ctx,
        "ctxT": ctx.reshape(-1, D).T,
        "idx": a['itok_BxS_0_255'],
        "mask": a['mask_BxS2_if1'],
        "w_qk": _np.stack([heads(a['L0_xattn_Wq']).T, heads(a['L0_xattn_Wk']).T], axis=1),
        "w_rest": _np.stack([a[n].T for n in _WEIGHTS], axis=1),
        "cols": _np.concatenate([heads(a['L0_xattn_bq']), heads(a['L0_xattn_bk'])] + [a[n][:, None] for n in _COLS], axis=1),
        "rows": _np.stack([a[n] for n in _ROWS]),
    }

    nc = _bacc.Bacc("TRN2", target_bir_lowering=False, num_devices=1)
    arrays, args = {}, []
    for name, v in laid_out.items():
        v = _np.ascontiguousarray(v)
        arrays[f"in_{name}_dram"] = v
        args.append(nc.dram_tensor(f"in_{name}_dram", v.shape, _mybir.dt.from_np(v.dtype), kind="ExternalInput").ap())
    args.append(nc.dram_tensor("out_0_dram", shape, _mybir.dt.float32, kind="ExternalOutput").ap())
    xattn_kernel(nc, *args)
    r = _run(nc, [arrays], core_ids=[0])
    return r.results[0]["out_0_dram"]
```
